# Optimizing a Trainium2 kernel written in Bass

```python
import numpy as np
import jax
import jax.numpy as jnp

def _softmax(x, axis=-1):
    return jax.nn.softmax(x, axis=axis)

def _gelu(x):
    return jax.nn.gelu(x, approximate=True)

def _silu(x):
    return jax.nn.silu(x)

def _sigmoid(x):
    return jax.nn.sigmoid(x)

def _layernorm(x, axis=-1, eps=1e-05):
    m = jnp.mean(x, axis=axis, keepdims=True)
    v = jnp.var(x, axis=axis, keepdims=True)
    return (x - m) / jnp.sqrt(v + eps)

def _scatter_add(tgt, idx, src, axis=0):
    return tgt.at[idx].add(src)

def _segment_sum(src, seg, n):
    return jax.ops.segment_sum(src, seg, n)
kernel_name = 'mk_xattn_ffn_d1_seqx_r8_d2ed59'

def setup_inputs(seed: int=0):
    np.random.seed(seed)
    _w = jnp.asarray

    def _rec_inputs():
        import jax
        import jax.numpy as jnp
        _rk = jax.random.key(seed)
        x = 7.22e-05 + 1 * jax.random.normal(jax.random.fold_in(_rk, 1), (8, 128, 256), jnp.float32)
        _lenS = 128 - jax.random.randint(jax.random.fold_in(_rk, 7), (8,), 0, max(1, 128 // 4) + 1, jnp.int32)
        _lenS2 = 128 - jax.random.randint(jax.random.fold_in(_rk, 8), (8,), 0, max(1, 128 // 4) + 1, jnp.int32)
        _ctx_2048P = jax.random.normal(jax.random.fold_in(_rk, 11), (8, 16, 256), jnp.float32)
        _ctx_2048c = jax.random.dirichlet(jax.random.fold_in(_rk, 511), 0.3 * jnp.ones((16,), jnp.float32), (8, 128))
        _ctx_2048t = jnp.einsum('bsk,bkd->bsd', _ctx_2048c, _ctx_2048P)
        _ctx_2048t = _ctx_2048t * jax.lax.rsqrt(jnp.mean(jnp.square(_ctx_2048t)) + 1e-12) * 0.953939
        ctx_2048 = 4.13588e-05 + 0.999923 * (_ctx_2048t + 0.3 * jax.random.normal(jax.random.fold_in(_rk, 611), (8, 128, 256), jnp.float32))
        return (x, ctx_2048)
    x, ctx_2048 = _rec_inputs()

    def _L0_xattn_setup():
        import jax, jax.numpy as jnp
        import numpy as np
        import math
        EMBED = 256
        HEADS = 32
        GROUPS = 8
        GROUP_HEADS = HEADS // GROUPS
        HEAD_DIM = EMBED // HEADS
        B, S = (4, 128)
        key = jax.random.key(seed)
        ks = jax.random.split(key, 8)
        sc = 0.02
        return {'q': jax.random.normal(ks[0], (B, S, EMBED), jnp.float32), 'k': jax.random.normal(ks[1], (B, S, EMBED), jnp.float32), 'v': jax.random.normal(ks[2], (B, S, EMBED), jnp.float32), 'Wq': jax.random.normal(ks[3], (EMBED, EMBED), jnp.float32) * sc, 'Wk': jax.random.normal(ks[4], (GROUPS * HEAD_DIM, EMBED), jnp.float32) * sc, 'Wv': jax.random.normal(ks[5], (GROUPS * HEAD_DIM, EMBED), jnp.float32) * sc, 'Wfc': jax.random.normal(ks[6], (EMBED, EMBED), jnp.float32) * sc, 'bfc': jnp.zeros((EMBED,), jnp.float32)}
    _L0_xattn_all = _L0_xattn_setup()
    _L0_xattn_in = {k: v for k, v in _L0_xattn_all.items() if k in ('Wq', 'Wk', 'Wv', 'Wfc', 'bfc')}
    del _L0_xattn_all

    def _L0_ffn_setup():
        import jax, jax.numpy as jnp
        import numpy as np
        B, T, D, E, F, K, ND = (2, 32, 256, 64, 64, 4, 4)
        H = F * K
        N_SHARED = 2
        key = jax.random.key(seed)
        ks = jax.random.split(key, 12)
        s = lambda k, shape: jax.random.normal(k, shape, jnp.float32) * 0.02
        x = jax.random.normal(ks[0], (B, T, D), jnp.float32)
        Wr = s(ks[1], (E, D))
        router_bias = jnp.zeros((E,), jnp.float32)
        affinity = s(ks[2], (E, ND))
        te_W1 = s(ks[3], (D // 2, D))
        te_b1 = jnp.zeros((D // 2,), jnp.float32)
        te_W2 = s(ks[4], (ND, D // 2))
        te_b2 = jnp.zeros((ND,), jnp.float32)
        Wg = s(ks[5], (E, D, F))
        Wu = s(ks[6], (E, D, F))
        Wd = s(ks[7], (E, F, D))
        Sg = s(ks[8], (N_SHARED, D, H))
        Su = s(ks[9], (N_SHARED, D, H))
        Sd = s(ks[10], (N_SHARED, H, D))
        return dict(x=x, Wr=Wr, router_bias=router_bias, affinity=affinity, te_W1=te_W1, te_b1=te_b1, te_W2=te_W2, te_b2=te_b2, Wg=Wg, Wu=Wu, Wd=Wd, Sg=Sg, Su=Su, Sd=Sd)
    _L0_ffn_all = _L0_ffn_setup()
    _L0_ffn_in = {k: v for k, v in _L0_ffn_all.items() if k in ('Wr', 'router_bias', 'affinity', 'te_W1', 'te_b1', 'te_W2', 'te_b2', 'Wg', 'Wu', 'Wd', 'Sg', 'Su', 'Sd')}
    del _L0_ffn_all
    return {'x': x, 'ctx_2048': ctx_2048, 'L0_xattn_Wq': _L0_xattn_in['Wq'], 'L0_xattn_Wk': _L0_xattn_in['Wk'], 'L0_xattn_Wv': _L0_xattn_in['Wv'], 'L0_xattn_Wfc': _L0_xattn_in['Wfc'], 'L0_xattn_bfc': _L0_xattn_in['bfc'], 'L0_ffn_Wr': _L0_ffn_in['Wr'], 'L0_ffn_router_bias': _L0_ffn_in['router_bias'], 'L0_ffn_affinity': _L0_ffn_in['affinity'], 'L0_ffn_te_W1': _L0_ffn_in['te_W1'], 'L0_ffn_te_b1': _L0_ffn_in['te_b1'], 'L0_ffn_te_W2': _L0_ffn_in['te_W2'], 'L0_ffn_te_b2': _L0_ffn_in['te_b2'], 'L0_ffn_Wg': _L0_ffn_in['Wg'], 'L0_ffn_Wu': _L0_ffn_in['Wu'], 'L0_ffn_Wd': _L0_ffn_in['Wd'], 'L0_ffn_Sg': _L0_ffn_in['Sg'], 'L0_ffn_Su': _L0_ffn_in['Su'], 'L0_ffn_Sd': _L0_ffn_in['Sd']}

def reference(x, ctx_2048, L0_xattn_Wq, L0_xattn_Wk, L0_xattn_Wv, L0_xattn_Wfc, L0_xattn_bfc, L0_ffn_Wr, L0_ffn_router_bias, L0_ffn_affinity, L0_ffn_te_W1, L0_ffn_te_b1, L0_ffn_te_W2, L0_ffn_te_b2, L0_ffn_Wg, L0_ffn_Wu, L0_ffn_Wd, L0_ffn_Sg, L0_ffn_Su, L0_ffn_Sd):
    import jax
    import jax.numpy as jnp

    def _L0_xattn_ref(q, k, v, Wq, Wk, Wv, Wfc, bfc):
        import jax, jax.numpy as jnp
        import numpy as np
        import math
        EMBED = 256
        HEADS = 32
        GROUPS = 8
        GROUP_HEADS = HEADS // GROUPS
        HEAD_DIM = EMBED // HEADS
        B, S = (4, 128)
        N, S_, _ = q.shape
        qh = (q @ Wq.T).reshape(N, S_, HEADS, HEAD_DIM).transpose(0, 2, 1, 3)
        kh = (k @ Wk.T).reshape(N, S_, GROUPS, HEAD_DIM).transpose(0, 2, 1, 3)
        vh = (v @ Wv.T).reshape(N, S_, GROUPS, HEAD_DIM).transpose(0, 2, 1, 3)
        kh = jnp.repeat(kh, GROUP_HEADS, axis=1)
        vh = jnp.repeat(vh, GROUP_HEADS, axis=1)
        score = jnp.einsum('bhqd,bhkd->bhqk', qh, kh) / math.sqrt(HEAD_DIM)
        attn = jax.nn.softmax(score, axis=-1)
        out = jnp.einsum('bhqk,bhkd->bhqd', attn, vh)
        out = out.transpose(0, 2, 1, 3).reshape(N, S_, EMBED)
        return out @ Wfc.T + bfc

    def _L0_ffn_ref(x, Wr, router_bias, affinity, te_W1, te_b1, te_W2, te_b2, Wg, Wu, Wd, Sg, Su, Sd):
        import jax, jax.numpy as jnp
        import numpy as np
        B, T, D, E, F, K, ND = (2, 32, 256, 64, 64, 4, 4)
        H = F * K
        N_SHARED = 2
        b, t, d = x.shape
        n = b * t
        flat = x.reshape(n, d)
        xm = x.mean(axis=1)
        h1 = jax.nn.gelu(xm @ te_W1.T + te_b1, approximate=False)
        task_dist = jax.nn.softmax(h1 @ te_W2.T + te_b2, axis=-1)
        dom = task_dist @ affinity.T
        logits = (flat @ Wr.T).reshape(b, t, E) + 0.5 * dom[:, None, :]
        logits = logits.reshape(n, E)
        scores = jax.nn.softmax(logits, axis=-1)
        _, topk_idx = jax.lax.top_k(logits + router_bias, K)
        topk_scores = jnp.take_along_axis(scores, topk_idx, axis=-1)
        topk_scores = topk_scores / (topk_scores.sum(-1, keepdims=True) + 1e-08)
        combine = jnp.zeros((n, E), x.dtype).at[jnp.arange(n)[:, None], topk_idx].add(topk_scores)
        g = jnp.einsum('nd,edf->enf', flat, Wg)
        u = jnp.einsum('nd,edf->enf', flat, Wu)
        h = jax.nn.silu(g) * u
        hw = h * combine.T[:, :, None]
        out = jnp.einsum('enf,efd->nd', hw, Wd)
        for i in range(Sg.shape[0]):
            sh = jax.nn.silu(flat @ Sg[i]) * (flat @ Su[i])
            out = out + sh @ Sd[i]
        return out.reshape(b, t, d)
    x = x + _L0_xattn_ref(_layernorm(x, axis=-1), ctx_2048, ctx_2048, L0_xattn_Wq, L0_xattn_Wk, L0_xattn_Wv, L0_xattn_Wfc, L0_xattn_bfc)
    x = x + _L0_ffn_ref(_layernorm(x, axis=-1), L0_ffn_Wr, L0_ffn_router_bias, L0_ffn_affinity, L0_ffn_te_W1, L0_ffn_te_b1, L0_ffn_te_W2, L0_ffn_te_b2, L0_ffn_Wg, L0_ffn_Wu, L0_ffn_Wd, L0_ffn_Sg, L0_ffn_Su, L0_ffn_Sd)
    return x

_drawn_inputs = setup_inputs


def setup_inputs(seed=0):
    import zlib

    import numpy as np

    out = dict(_drawn_inputs(seed))
    spreads = {'L0_xattn_bfc': (0.0, 0.1),
     'L0_ffn_router_bias': (0.0, 0.8),
     'L0_ffn_te_b1': (0.0, 2.0),
     'L0_ffn_te_b2': (0.0, 2.0)}
    factors = {'L0_xattn_Wq': 8.0,
     'L0_xattn_Wk': 8.0,
     'L0_ffn_Wr': 8.0,
     'L0_ffn_affinity': 23.091,
     'L0_ffn_te_W1': 30.016,
     'L0_ffn_te_W2': 23.507,
     'L0_ffn_Wg': 8.0,
     'L0_ffn_Wu': 8.0,
     'L0_ffn_Wd': 8.0,
     'L0_ffn_Sg': 8.0,
     'L0_ffn_Su': 8.0,
     'L0_ffn_Sd': 8.0}
    for name, (base, spread) in spreads.items():
        noise = np.random.default_rng([zlib.crc32(name.encode()), seed]).standard_normal(out[name].shape)
        drawn = base * np.exp(spread * noise) if base else spread * noise
        out[name] = jnp.asarray(drawn.astype(out[name].dtype))
    for name, factor in factors.items():
        out[name] = (out[name] * factor).astype(out[name].dtype)
    return out
```

```python
from contextlib import ExitStack

import concourse.bass as bass
from concourse import mybir

F32 = mybir.dt.float32
F32R = mybir.dt.float32r
ACT = mybir.ActivationFunctionType
ALU = mybir.AluOpType
AX_X = mybir.AxisListType.X

P = 128
B, T, D = 8, 128, 256
NC = D // P
HEADS, GROUPS = 32, 8
J = HEADS // GROUPS
HD = D // HEADS
STRIP = 32
SG = P // STRIP
NG = GROUPS // SG
E, F = 64, 64
TOPK = 4
H_SHARED = 256
N_SHARED = 2
ND = 4
TOK = B * T
HALF = TOK // 2
SHARED_UNITS = N_SHARED * H_SHARED // P
EXPERT_UNITS = E * F // P
UNITS = SHARED_UNITS + EXPERT_UNITS
EPS = 1e-5
SCALE = float(HD) ** -0.5
GUARD = 1e-8
FAR = 3.0e38


def build(nc, x, ctx, Wq, Wk, Wv, Wfc, bfc, Wr, rbias, aff, W1, b1, W2, b2, Wg, Wu, Wd, Sg, Su, Sd,
          ident_d, onesel_d, jmask_d, out):
    c_dram = nc.dram_tensor("combine_scratch", (E, TOK), F32, kind="Internal").ap()
    with ExitStack() as stack:
        def sb(name, shape, dt=F32):
            return stack.enter_context(nc.sbuf_tensor(name, shape, dt))

        def sem(name):
            return stack.enter_context(nc.semaphore(name))

        bank = [stack.enter_context(nc.psum_tensor(f"bank{i}", [P, 512], F32)) for i in range(8)]
        S_ps, ST_ps, O_ps, MA, MB = bank[0:2], bank[2:4], bank[4:6], bank[6], bank[7]
        G_ps, U_ps = bank[0], bank[1]
        ACC = [bank[2:4], bank[4:6]]

        ident = sb("ident", [P, P])
        onesel_raw = sb("onesel_raw", [2 * HEADS, GROUPS * P])
        onesel = sb("onesel", [2 * HEADS, GROUPS * P], F32R)
        jmask = sb("jmask", [2 * HEADS, J])
        inv_t = sb("inv_t", [P, 2])
        wq_n = sb("wq_n", [P, NC, D])
        wfc_n = sb("wfc_n", [P, NC, D])
        wkv_n = sb("wkv_n", [P, D])
        wr_n = sb("wr_n", [E, D])
        w1_n = sb("w1_n", [P, D])
        w2_n = sb("w2_n", [ND, P])
        aff_n = sb("aff_n", [E, ND])
        wqT = sb("wqT", [P, NC * D])
        wfcT = sb("wfcT", [P, NC * D])
        wkvT = sb("wkvT", [P, NC * P])
        wrT = sb("wrT", [P, NC * E])
        wrT_hi = sb("wrT_hi", [P, NC * E], F32R)
        wrT_lo = sb("wrT_lo", [P, NC * E], F32R)
        w1T = sb("w1T", [P, NC * P])
        w2T = sb("w2T", [P, ND])
        affT = sb("affT", [ND, E])
        bfc_b = sb("bfc_b", [P, D])
        b1_c = sb("b1_c", [P, 1])
        b2_b = sb("b2_b", [B, ND])
        rbias_b = sb("rbias_b", [P, E])

        x_all = sb("x_all", [P, B * D])
        ctx_in = [sb(f"ctx_in{i}", [P, D]) for i in range(2)]
        xb_all = sb("xb_all", [P, B * D])
        stats = [sb(f"stats{i}", [P, B * 6]) for i in range(2)]
        mv = [sb(f"mv{i}", [P, B * 2]) for i in range(2)]
        var = [sb(f"var{i}", [P, B]) for i in range(2)]
        std = [sb(f"std{i}", [P, B]) for i in range(2)]
        rstd = [sb(f"rstd{i}", [P, B]) for i in range(2)]
        newton = sb("newton", [P, B])
        xn = sb("xn", [P, D])
        xcT = sb("xcT", [P, 2 * D])
        qrep = sb("qrep", [P, HEADS * STRIP], F32R)
        krep = sb("krep", [P, GROUPS * STRIP], F32R)
        qT = [sb(f"qT{i}", [P, NG * J * T], F32R) for i in range(2)]
        kT = [sb(f"kT{i}", [P, NG * SG * T], F32R) for i in range(2)]
        Vw = [sb(f"Vw{i}", [P, GROUPS * STRIP]) for i in range(2)]
        v_sb = sb("v_sb", [P, GROUPS * HD])
        mx = [sb(f"mx{i}", [P, HEADS]) for i in range(2)]
        ml = sb("ml", [P, 2, HEADS, 2], F32R)
        Dm = sb("Dm", [2 * HEADS, J * T], F32R)
        Pr = [sb(f"Pr{g}", [P, J * T]) for g in range(GROUPS)]
        O_sb = [sb(f"O_sb{i}", [P, J * T]) for i in range(NG)]
        rec = sb("rec", [P, NG, J * SG])
        attn = sb("attn", [P, D])
        attnT = sb("attnT", [P, D])
        x2n = [sb(f"x2n{i}", [P, D]) for i in range(2)]
        x2hi = sb("x2hi", [P, NC, TOK], F32R)
        x2lo = sb("x2lo", [P, NC, TOK], F32R)
        xmT = sb("xmT", [P, NC, B])

        h1T = sb("h1T", [P, B])
        td = sb("td", [B, ND])
        tdm = sb("tdm", [B, 1])
        tds = sb("tds", [B, 1])
        tdr = sb("tdr", [B, 1])
        tdn = sb("tdn", [B, ND])
        tdT = sb("tdT", [ND, B])
        tdb = sb("tdb", [ND, B * T])
        lg = sb("lg", [P, B, E])
        lb = sb("lb", [P, B, E + 8])
        top = sb("top", [P, B, 8])
        rep = sb("rep", [P, B, E + 8])
        sel = sb("sel", [P, B, E])
        lmax = sb("lmax", [P, B])
        ex = sb("ex", [P, B, E])
        z_all = sb("z_all", [P, B])
        z_top = sb("z_top", [P, B])
        cw = sb("cw", [P, B, E])
        cT = sb("cT", [E, TOK])

        raw = [sb(f"raw{i}", [P, 3 * D]) for i in range(2)]
        whi = [sb(f"whi{i}", [P, 3 * D], F32R) for i in range(2)]
        wlo = [sb(f"wlo{i}", [P, 3 * D], F32R) for i in range(2)]
        cb = [sb(f"cb{i}", [P, TOK]) for i in range(2)]
        sil = [sb(f"sil{i}", [P, HALF]) for i in range(2)]
        su = [sb(f"su{i}", [P, HALF]) for i in range(2)]
        hh = [sb(f"hh{i}", [P, HALF]) for i in range(2)]
        hhi = [sb(f"hhi{i}", [P, HALF], F32R) for i in range(2)]
        hlo = [sb(f"hlo{i}", [P, HALF], F32R) for i in range(2)]
        yT = sb("yT", [P, NC, TOK])
        y = sb("y", [P, B * D])

        NW = ["ident", "wq", "wkv", "onesel", "jmask", "wfc", "wr", "w1", "w2", "aff", "bfc", "b1", "b2", "rbias"]
        arrived = {n: sem(f"arrived_{n}") for n in NW}
        x_first, x_rest = sem("x_first"), sem("x_rest")
        ctx_arrived = [sem(f"ctx_arrived{i}") for i in range(2)]
        raw_in = [sem(f"raw_in{i}") for i in range(2)]
        cb_in = [sem(f"cb_in{i}") for i in range(2)]
        c_out = sem("c_out")
        y_out = sem("y_out")
        pe_w = sem("pe_w")
        pe_T1, pe_PJ, pe_QKT, pe_S, pe_MT, pe_ST, pe_PV, pe_OT, pe_AT, pe_FC, pe_XT = (
            sem(f"pe_{n}") for n in ("T1", "PJ", "QKT", "S", "MT", "ST", "PV", "OT", "AT", "FC", "XT"))
        pe_h1, pe_td, pe_tdT, pe_logits, pe_cT = (sem(f"pe_{n}") for n in ("h1", "td", "tdT", "logits", "cT"))
        pe_G, pe_U, pe_D, pe_Y = (sem(f"pe_{n}") for n in ("G", "U", "D", "Y"))
        a_w, a_std, a_xcT, a_qkv, a_kT, a_qT, a_exp, a_O, a_attnT, a_x2hi = (
            sem(f"a_{n}") for n in ("w", "std", "xcT", "qkv", "kT", "qT", "exp", "O", "attnT", "x2hi"))
        a_h1, a_td, a_ex, a_sil, a_hhi, a_whi, a_yT = (sem(f"a_{n}") for n in ("h1", "td", "ex", "sil", "hhi", "whi", "yT"))
        (v_w, v_const, v_stat, v_ln, v_ln2, v_xn, v_lo, v_qT, v_max, v_mhi, v_ml, v_D, v_rec, v_norm, v_x2,
         v_stat2, v_x2n, v_x2lo) = (
            sem(f"v_{n}") for n in ("w", "const", "stat", "ln", "ln2", "xn", "lo", "qT", "max", "mhi", "ml",
                                    "D", "rec", "norm", "x2", "stat2", "x2n", "x2lo"))
        v_gate, v_su, v_h, v_hlo, v_yT, v_y = (sem(f"v_{n}") for n in ("gate", "su", "h", "hlo", "yT", "y"))
        g_const, g_zero, g_xb, g_V, g_wlo = (sem(f"g_{n}") for n in ("const", "zero", "xb", "V", "wlo"))

        FIRST_N, LAST_N = -2, B
        LOOP = (2, 6)

        def iterations(eng, body):
            def has(k):
                return 0 <= k < B
            for n in range(FIRST_N, LOOP[0]):
                body(n, n % 2, has)
            with eng.Fori(LOOP[0] // 2, LOOP[1] // 2) as t:
                n = 2 * t
                body(n, 0, lambda k: True)
                body(n + 1, 1, lambda k: True)
            for n in range(LOOP[1], LAST_N + 1):
                body(n, n % 2, has)

        SCORES_AT = ((), (0,), (1, 2), (3,), (4, 5), (6,), (7,), ())

        def wait(eng, s, value):
            if isinstance(value, int) and value <= 0:
                return
            eng.wait_ge(s, value)

        block = stack.enter_context(nc.Block())

        @block.sync
        def _(sp):
            sp.dma_start(x_all[:, 0:D], x[0]).then_inc(x_first, 16)
            sp.dma_start(ident[:], ident_d).then_inc(arrived["ident"], 16)
            sp.dma_start(ctx_in[0][:], ctx[0]).then_inc(ctx_arrived[0], 16)
            sp.dma_start(wq_n[:], Wq.rearrange("(a p) i -> p a i", p=P)).then_inc(arrived["wq"], 16)
            sp.dma_start(wkv_n[0:64, :], Wk).then_inc(arrived["wkv"], 16)
            sp.dma_start(wkv_n[64:128, :], Wv).then_inc(arrived["wkv"], 16)
            sp.dma_start(x_all[:, D:].rearrange("p (b d) -> p b d", b=B - 1),
                         x[1:B].rearrange("b p d -> p b d")).then_inc(x_rest, 16)
            sp.dma_start(ctx_in[1][:], ctx[1]).then_inc(ctx_arrived[1], 16)
            sp.dma_start(onesel_raw[:], onesel_d).then_inc(arrived["onesel"], 16)
            sp.dma_start(jmask[:], jmask_d).then_inc(arrived["jmask"], 16)
            sp.dma_start(wfc_n[:], Wfc.rearrange("(a p) i -> p a i", p=P)).then_inc(arrived["wfc"], 16)
            sp.dma_start(wr_n[:], Wr).then_inc(arrived["wr"], 16)
            sp.dma_start(w1_n[:], W1).then_inc(arrived["w1"], 16)
            sp.dma_start(w2_n[:], W2).then_inc(arrived["w2"], 16)
            sp.dma_start(aff_n[:], aff).then_inc(arrived["aff"], 16)
            sp.dma_start(bfc_b[:], bfc.rearrange("(a n) -> a n", a=1).broadcast_to([P, D])).then_inc(arrived["bfc"], 16)
            sp.dma_start(b1_c[:], b1.rearrange("(p a) -> p a", a=1)).then_inc(arrived["b1"], 16)
            sp.dma_start(b2_b[:], b2.rearrange("(a n) -> a n", a=1).broadcast_to([B, ND])).then_inc(arrived["b2"], 16)
            sp.dma_start(rbias_b[:], rbias.rearrange("(a n) -> a n", a=1).broadcast_to([P, E])).then_inc(arrived["rbias"], 16)

            def load_unit(i, gate_up, down):
                for m in range(2):
                    dst = raw[i][:, m * D:(m + 1) * D]
                    src = gate_up[m]
                    if len(src.shape) == 4:
                        sp.dma_start(dst.rearrange("p (e c f) -> p e c f", e=2, c=NC), src).then_inc(raw_in[i], 16)
                    else:
                        sp.dma_start(dst.rearrange("p (c f) -> p c f", c=NC), src).then_inc(raw_in[i], 16)
                sp.dma_start(raw[i][:, 2 * D:3 * D], down).then_inc(raw_in[i], 16)

            def shared(u):
                s, h = divmod(u, H_SHARED // P)
                cols = slice(h * P, (h + 1) * P)
                return ([w[s, :, cols].rearrange("(p c) f -> p c f", c=NC) for w in (Sg, Su)],
                        Sd[s, h * P:(h + 1) * P, :])

            def experts(u):
                e = 2 * (u - SHARED_UNITS)
                return ([w[bass.ds(e, 2)].rearrange("e (p c) f -> p e c f", c=NC) for w in (Wg, Wu)],
                        Wd.rearrange("e f d -> (e f) d")[bass.ds(e * F, P), :])

            def load_combine(i, u):
                e = 2 * (u - SHARED_UNITS)
                for k in range(2):
                    sp.dma_start(cb[i][k * F:(k + 1) * F, :],
                                 c_dram[bass.ds(e + k, 1), :].broadcast_to([F, TOK])).then_inc(cb_in[i], 16)

            for u in range(2):
                load_unit(u, *shared(u))
            with sp.Fori(1, B // 2) as t:
                for i in range(2):
                    sp.wait_ge(pe_T1, 2 * t + i - 1)
                    sp.dma_start(ctx_in[i][:], ctx.rearrange("b p d -> (b p) d")[bass.ds((2 * t + i) * P, P), :])\
                      .then_inc(ctx_arrived[i], 16)
            for u in range(2, SHARED_UNITS):
                sp.wait_ge(g_wlo, u - 1)
                load_unit(u % 2, *shared(u))
            for u in range(SHARED_UNITS, SHARED_UNITS + 2):
                wait(sp, g_wlo, u - 1)
                load_unit(u % 2, *experts(u))
            sp.wait_ge(v_gate, GATE_STEPS)
            sp.dma_start(c_dram, cT[:]).then_inc(c_out, 16)
            sp.wait_ge(c_out, 16)
            for u in range(SHARED_UNITS, SHARED_UNITS + 2):
                load_combine(u % 2, u)
            with sp.Fori((SHARED_UNITS + 2) // 2, (UNITS) // 2) as t:
                u = 2 * t
                for i in range(2):
                    sp.wait_ge(g_wlo, u + i - 1)
                    load_unit(i, *experts(u + i))
                    sp.wait_ge(v_h, 2 * (u + i) - 2)
                    load_combine(i, u + i)
            for q in range(4):
                sp.wait_ge(v_y, q + 1)
                sp.dma_start(out[2 * q:2 * q + 2].rearrange("b p d -> p b d"),
                             y[:, 2 * q * D:(2 * q + 2) * D].rearrange("p (b d) -> p b d", b=2)).then_inc(y_out, 16)
            sp.wait_ge(y_out, 64)

        @block.gpsimd
        def _(pool):
            for i in range(2):
                nc.gpsimd.memset(Vw[i][:], 1.0).then_inc(g_const, 1)
            for i in range(2):
                nc.gpsimd.memset(kT[i][:].bitcast(F32), 0.0).then_inc(g_zero, 1)
            nc.gpsimd.memset(ml[:, 1].bitcast(F32), 0.0).then_inc(g_const, 1)
            nc.gpsimd.memset(inv_t[:], 1.0 / T).then_inc(g_const, 1)
            nc.gpsimd.memset(lb[:, :, E:E + 8], FAR).then_inc(g_const, 1)
            pool.wait_ge(x_first, 16)
            pool.wait_ge(x_rest, 16)
            pool.wait_ge(arrived["bfc"], 16)
            for b in range(B):
                nc.gpsimd.tensor_tensor(xb_all[:, b * D:(b + 1) * D], x_all[:, b * D:(b + 1) * D], bfc_b[:],
                                        ALU.add).then_inc(g_xb, 1)

            def place_V(k, i):
                pool.wait_ge(a_qkv, k + 1)
                wait(pool, pe_PV, 2 * k - 2)
                nc.gpsimd.tensor_copy(Vw[i][:].rearrange("p (g r) -> p g r", g=GROUPS)[:, :, 0:HD],
                                      v_sb[:].rearrange("p (g d) -> p g d", g=GROUPS)).then_inc(g_V, 1)

            pool.wait_ge(g_const, 2)
            for k in range(B):
                place_V(k, k % 2)

            def split(i, u, n_raw, pairs):
                pool.wait_ge(raw_in[i], n_raw)
                pool.wait_ge(a_whi, 2 * u + 1)
                wait(pool, pe_U, 2 * u - 2)
                gu_lo = wlo[i][:, 0:2 * D]
                gu_hi = whi[i][:, 0:2 * D].bitcast(F32)
                gu = raw[i][:, 0:2 * D]
                if pairs:
                    for m in range(2):
                        s = slice(m * D, (m + 1) * D)
                        order = "p (e c f) -> p c e f"
                        nc.gpsimd.tensor_tensor(wlo[i][:, s].rearrange("p (c e f) -> p c e f", c=NC, e=2),
                                                raw[i][:, s].rearrange(order, c=NC, e=2),
                                                whi[i][:, s].bitcast(F32).rearrange("p (c e f) -> p c e f", c=NC, e=2),
                                                ALU.subtract)
                else:
                    nc.gpsimd.tensor_tensor(gu_lo, gu, gu_hi, ALU.subtract)
                pool.wait_ge(a_whi, 2 * u + 2)
                wait(pool, pe_D, 2 * u - 2)
                nc.gpsimd.tensor_tensor(wlo[i][:, 2 * D:3 * D], raw[i][:, 2 * D:3 * D],
                                        whi[i][:, 2 * D:3 * D].bitcast(F32), ALU.subtract).then_inc(g_wlo, 1)

            for u in range(SHARED_UNITS):
                split(u % 2, u, 48 * (u // 2 + 1), False)
            with pool.Fori((SHARED_UNITS) // 2, (UNITS) // 2) as t:
                u = 2 * t
                for i in range(2):
                    split(i, u + i, 24 * u + 48, True)

        @block.scalar
        def _(act):
            copy, exp = ACT.Copy, ACT.Exp
            act.wait_ge(v_ln, 1)
            nc.scalar.activation(std[0][:], var[0][:], ACT.Sqrt).then_inc(a_std, 1)
            act.wait_ge(pe_w, 2)
            nc.scalar.activation(wfcT[:], bank[1][:], copy).then_inc(a_w, 1)

            def body(n, odd, has):
                if has(n + 1):
                    k = n + 1
                    act.wait_ge(pe_QKT, 3 * k + 1)
                    wait(act, pe_ST, 8 * k - 8)
                    if isinstance(k, int) and k < 2:
                        act.wait_ge(g_zero, k + 1)
                    for s in range(SG):
                        last = nc.scalar.activation(
                            kT[1 - odd][s * STRIP:(s + 1) * STRIP, :].rearrange("p (G s t) -> p G s t", G=NG, s=SG)[:, :, s, :],
                            S_ps[0][s * STRIP:(s + 1) * STRIP, 0:NG * T].rearrange("p (G t) -> p G t", G=NG), copy)
                    last.then_inc(a_kT, 1)
                    act.wait_ge(pe_QKT, 3 * k + 2)
                    nc.scalar.activation(qT[1 - odd][:, 0:J * T], MA[:], copy).then_inc(a_qT, 1)
                for g in range(GROUPS):
                    if has(n):
                        act.wait_ge(pe_ST, 8 * n + g + 1)
                        wait(act, pe_PV, 2 * n - 1 + g // SG)
                        nc.scalar.activation(Pr[g][:], ST_ps[g % 2][:], exp, scale=SCALE).then_inc(a_exp, 1)
                    if g == 0 and has(n - 1):
                        evac_O(n - 1, 1)
                    if g == 3 and has(n + 2):
                        k = n + 2
                        act.wait_ge(pe_T1, k + 1)
                        wait(act, pe_PJ, k)
                        nc.scalar.activation(xcT[:], MB[:], copy).then_inc(a_xcT, 1)
                    if g == 4 and has(n - 1):
                        act.wait_ge(pe_AT, n)
                        wait(act, pe_FC, n - 1)
                        nc.scalar.activation(attnT[:], MB[:, 0:D], copy).then_inc(a_attnT, 1)
                    if g == 5 and has(n + 2):
                        k = n + 2
                        act.wait_ge(pe_PJ, k + 1)
                        wait(act, pe_QKT, 3 * k)
                        wait(act, g_V, k)
                        nc.scalar.activation(v_sb[:], MA[:, D + 64:D + 128], copy)
                        kv = krep[:].rearrange("p (g r d) -> p g r d", g=GROUPS, r=4)
                        nc.scalar.activation(kv[:, :, 0:2, :],
                                             MA[:, D:D + 64].rearrange("p (g a d) -> p g a d", g=GROUPS, a=1)
                                             .broadcast_to([P, GROUPS, 2, HD]), copy)
                        qv = qrep[:].rearrange("p (h r d) -> p h r d", h=HEADS, r=4)
                        nc.scalar.activation(qv[:, :, 0:4:2, :],
                                             MA[:, 0:D].rearrange("p (h a d) -> p h a d", h=HEADS, a=1)
                                             .broadcast_to([P, HEADS, 2, HD]), copy).then_inc(a_qkv, 1)
                    if g == 6 and has(n):
                        evac_O(n, 0)

            def evac_O(k, G):
                act.wait_ge(pe_PV, 2 * k + G + 1)
                wait(act, pe_OT, 2 * k - 1 + G)
                nc.scalar.activation(O_sb[G][:], O_ps[G][:], copy).then_inc(a_O, 1)

            iterations(act, body)

            act.wait_ge(v_ln2, 1)
            nc.scalar.activation(std[1][:], var[1][:], ACT.Sqrt).then_inc(a_std, 1)
            for k in range(B):
                m = bank[k % 4]
                act.wait_ge(pe_XT, k + 1)
                nc.scalar.activation(xmT[:, :, k:k + 1], m[:, D:D + NC].rearrange("p (c a) -> p c a", a=1), copy)
                nc.scalar.activation(x2hi[:, :, k * T:(k + 1) * T], m[:, 0:D].rearrange("p (c t) -> p c t", c=NC),
                                     copy).then_inc(a_x2hi, 1)

            def weights_hi(i, u, n_raw, pairs):
                act.wait_ge(raw_in[i], n_raw)
                wait(act, pe_U, 2 * u - 2)
                for m in range(2):
                    s = slice(m * D, (m + 1) * D)
                    if pairs:
                        ins = nc.scalar.activation(whi[i][:, s].rearrange("p (c e f) -> p c e f", c=NC, e=2),
                                                   raw[i][:, s].rearrange("p (e c f) -> p c e f", c=NC, e=2), copy)
                    else:
                        ins = nc.scalar.activation(whi[i][:, s], raw[i][:, s], copy)
                ins.then_inc(a_whi, 1)
                wait(act, pe_D, 2 * u - 2)
                nc.scalar.activation(whi[i][:, 2 * D:], raw[i][:, 2 * D:], copy).then_inc(a_whi, 1)

            def silu(v, half):
                act.wait_ge(pe_G, v + 1)
                wait(act, v_su, v - 1)
                nc.scalar.activation(sil[half][:], G_ps[:], ACT.Silu).then_inc(a_sil, 1)

            def hidden_hi(v, half):
                act.wait_ge(v_h, v + 1)
                wait(act, pe_D, v - 1)
                nc.scalar.activation(hhi[half][:], hh[half][:], copy).then_inc(a_hhi, 1)

            weights_hi(0, 0, 48, False)
            act.wait_ge(pe_h1, 1)
            act.wait_ge(arrived["b1"], 16)
            nc.scalar.activation(h1T[:], MA[:, 0:B], ACT.Gelu, bias=b1_c[:, 0:1]).then_inc(a_h1, 1)
            for u in range(SHARED_UNITS):
                for half in range(2):
                    v = 2 * u + half
                    silu(v, half)
                    if half == 0:
                        if u + 1 < SHARED_UNITS:
                            weights_hi(1 - u % 2, u + 1, 48 * ((u + 1) // 2 + 1), False)
                        else:
                            weights_hi(0, u + 1, 24 * (u + 1) + 48, True)
                    if v == 1:
                        act.wait_ge(v_gate, 3)
                        nc.scalar.activation(td[:], td[:], exp, accum_out=tds[:, 0:1]).then_inc(a_td, 1)
                    if v == 4:
                        act.wait_ge(v_gate, GATE_EX)
                        nc.scalar.activation(ex[:], ex[:], exp).then_inc(a_ex, 1)
                    hidden_hi(v, half)
            with act.Fori((SHARED_UNITS) // 2, (UNITS - 2) // 2) as t:
                u = 2 * t
                for i in range(2):
                    for half in range(2):
                        v = 2 * (u + i) + half
                        silu(v, half)
                        if half == 0:
                            weights_hi(1 - i, u + i + 1, 24 * (u + 2 * i) + 48, True)
                        hidden_hi(v, half)
            for u in range(UNITS - 2, UNITS):
                for half in range(2):
                    silu(2 * u + half, half)
                    if half == 0 and u + 1 < UNITS:
                        weights_hi(1, u + 1, 24 * (UNITS - 2) + 48, True)
                    hidden_hi(2 * u + half, half)
            act.wait_ge(pe_D, 2 * UNITS)
            for half in range(2):
                nc.scalar.activation(yT[:, 0, half * HALF:(half + 1) * HALF], ACC[half][0][:], copy).then_inc(a_yT, 1)

        @block.vector
        def _(dve):
            nc.vector.memset(td[:], 0.0)
            dve.wait_ge(pe_w, 1)
            for cG in range(NC * NG):
                nc.vector.tensor_copy(wqT[:, cG * P:(cG + 1) * P].rearrange("p (j s d) -> p j s d", j=J, s=SG),
                                      bank[0][:, cG * P:(cG + 1) * P].rearrange("p (s j d) -> p j s d", j=J, s=SG))
            dve.wait_ge(pe_w, 3)
            nc.vector.tensor_copy(wkvT[:], bank[2][:, 0:NC * P]).then_inc(v_w, 1)
            dve.wait_ge(arrived["onesel"], 16)
            nc.vector.tensor_copy(onesel[:], onesel_raw[:]).then_inc(v_const, 1)

            def aggregate(i, done):
                for b in range(B):
                    last = nc.vector.bn_aggr(mv[i][:, 2 * b:2 * b + 2], stats[i][:, 6 * b:6 * b + 6])
                last.then_inc(done, 1)
                dve.wait_ge(done, B + 1)

            def inverse_deviation(i, done):
                v = mv[i][:].rearrange("p (b m) -> p b m", m=2)[:, :, 1]
                nc.vector.tensor_scalar(var[i][:], v, EPS, None, ALU.add).then_inc(done, 1)
                dve.wait_ge(a_std, i + 1)
                nc.vector.reciprocal(rstd[i][:], std[i][:]).then_inc(done, 1)
                dve.wait_ge(done, 2)
                nc.vector.tensor_tensor(newton[:], rstd[i][:], rstd[i][:], ALU.mult).then_inc(done, 1)
                dve.wait_ge(done, 3)
                nc.vector.tensor_tensor(newton[:], newton[:], var[i][:], ALU.mult).then_inc(done, 1)
                dve.wait_ge(done, 4)
                nc.vector.tensor_scalar(newton[:], newton[:], -0.5, 1.5, ALU.mult, ALU.add).then_inc(done, 1)
                dve.wait_ge(done, 5)
                nc.vector.tensor_tensor(rstd[i][:], rstd[i][:], newton[:], ALU.mult).then_inc(done, 1)
                dve.wait_ge(done, 6)

            def layernorm(i, src, k, dst, done):
                nc.vector.tensor_scalar(dst, src, mv[i][:, bass.ds(2 * k, 1)], rstd[i][:, bass.ds(k, 1)],
                                        ALU.subtract, ALU.mult).then_inc(done, 1)

            dve.wait_ge(x_first, 16)
            dve.wait_ge(x_rest, 16)
            for b in range(B):
                nc.vector.bn_stats(stats[0][:, 6 * b:6 * b + 6], x_all[:, b * D:(b + 1) * D]).then_inc(v_stat, 1)
            dve.wait_ge(v_stat, B)
            aggregate(0, v_stat)
            inverse_deviation(0, v_ln)

            def maximum(k, par, g):
                dve.wait_ge(pe_S, 8 * k + g + 1)
                nc.vector.tensor_reduce(mx[par][:, J * g:J * g + J], S_ps[g % 2][:].rearrange("p (j t) -> p j t", j=J),
                                        AX_X, ALU.max).then_inc(v_max, 1)

            def normalise(k, G):
                src = (MA, MB)[G][:].rearrange("p (j s r) -> p j s r", j=J, s=SG)
                dve.wait_ge(pe_OT, 2 * k + G + 1)
                r = rec[:, G, :].rearrange("p (j s a) -> p j s a", j=J, a=1)
                nc.vector.reciprocal(r, src[:, :, :, HD:HD + 1]).then_inc(v_rec, 1)
                dve.wait_ge(v_rec, 2 * k + G + 1)
                wait(dve, pe_AT, k)
                nc.vector.tensor_tensor(attn[:, G * P:(G + 1) * P].rearrange("p (s j d) -> p j s d", s=SG, j=J),
                                        src[:, :, :, 0:HD], r.broadcast_to([P, J, SG, HD]), ALU.mult).then_inc(v_norm, 1)

            def body(n, odd, has):
                k1 = n + 1
                if has(k1):
                    dve.wait_ge(pe_QKT, 3 * k1 + 3)
                    wait(dve, pe_ST, 8 * k1 - 8)
                    nc.vector.tensor_copy(qT[1 - odd][:, J * T:], MB[:]).then_inc(v_qT, 1)
                if has(n + 2):
                    k = n + 2
                    wait(dve, pe_T1, k)
                    layernorm(0, x_all[:, bass.ds(k * D, D)], k, xn[:], v_xn)
                for g in range(GROUPS):
                    if has(k1):
                        for i in SCORES_AT[g]:
                            maximum(k1, 1 - odd, i)
                    if g in (1, 2) and has(n - 1):
                        normalise(n - 1, g - 1)
                    if g == 5 and has(n + 2):
                        k = n + 2
                        dve.wait_ge(a_qkv, k + 1)
                        kv = krep[:].rearrange("p (g r d) -> p g r d", g=GROUPS, r=4)
                        nc.vector.tensor_tensor(kv[:, :, 2:4, :],
                                                MA[:, D:D + 64].rearrange("p (g a d) -> p g a d", g=GROUPS, a=1)
                                                .broadcast_to([P, GROUPS, 2, HD]), kv[:, :, 0:2, :].bitcast(F32), ALU.subtract)
                        qv = qrep[:].rearrange("p (h r d) -> p h r d", h=HEADS, r=4)
                        nc.vector.tensor_tensor(qv[:, :, 1:4:2, :],
                                                MA[:, 0:D].rearrange("p (h a d) -> p h a d", h=HEADS, a=1)
                                                .broadcast_to([P, HEADS, 2, HD]), qv[:, :, 0:4:2, :].bitcast(F32),
                                                ALU.subtract).then_inc(v_lo, 1)
                if has(k1):
                    dve.wait_ge(v_max, 8 * k1 + 8)
                    m = mx[1 - odd][:].rearrange("p (h a) -> p h a", a=1)
                    wait(dve, pe_MT, k1)
                    nc.vector.tensor_scalar(ml[:, 0, :, 0:1], m, -1.0, None, ALU.mult).then_inc(v_mhi, 1)
                    dve.wait_ge(v_mhi, k1 + 1)
                    nc.vector.scalar_tensor_tensor(out=ml[:, 0, :, 1:2], in0=m, scalar=-1.0, in1=ml[:, 0, :, 0:1].bitcast(F32),
                                                   op0=ALU.mult, op1=ALU.subtract).then_inc(v_ml, 1)
                if has(n - 1):
                    k = n - 1
                    dve.wait_ge(pe_FC, k + 1)
                    if isinstance(k, int) and k == 0:
                        dve.wait_ge(g_xb, B)
                    row = xb_all[:, bass.ds(k * D, D)]
                    nc.vector.tensor_tensor(row, MB[:, 0:D], row, ALU.add).then_inc(v_x2, 1)
                if has(k1):
                    dve.wait_ge(pe_MT, k1 + 1)
                    wait(dve, pe_ST, 8 * k1)
                    if isinstance(k1, int) and k1 == 0:
                        dve.wait_ge(arrived["jmask"], 16)
                    nc.vector.tensor_tensor(Dm[:].rearrange("p (j t) -> p j t", j=J),
                                            S_ps[1][0:2 * HEADS, 0:T].rearrange("p (a t) -> p a t", a=1).broadcast_to([2 * HEADS, J, T]),
                                            jmask[:].rearrange("p (j a) -> p j a", a=1).broadcast_to([2 * HEADS, J, T]),
                                            ALU.mult).then_inc(v_D, 1)
                if has(n - 1):
                    dve.wait_ge(v_x2, n)
                    nc.vector.bn_stats(stats[1][:, bass.ds(6 * (n - 1), 6)], row).then_inc(v_stat2, 1)
                if isinstance(n, int) and n == -2:
                    nc.vector.tensor_copy(wrT[:], bank[2][:, NC * P:NC * P + NC * E]).then_inc(v_w, 1)
                    dve.wait_ge(v_w, 2)
                    nc.vector.tensor_copy(wrT_hi[:], wrT[:]).then_inc(v_w, 1)
                    dve.wait_ge(v_w, 3)
                    nc.vector.tensor_tensor(wrT_lo[:], wrT[:], wrT_hi[:].bitcast(F32), ALU.subtract).then_inc(v_w, 1)
                    dve.wait_ge(pe_w, 4)
                    nc.vector.tensor_copy(w1T[:], bank[3][:, 0:NC * P])
                    nc.vector.tensor_copy(w2T[:], bank[3][:, NC * P:NC * P + ND])
                    nc.vector.tensor_copy(affT[:], bank[3][0:ND, NC * P + 64:NC * P + 64 + E]).then_inc(v_w, 1)

            iterations(dve, body)

            dve.wait_ge(v_stat2, B)
            aggregate(1, v_stat2)
            inverse_deviation(1, v_ln2)

            def x2_low(k):
                dve.wait_ge(a_x2hi, k + 1)
                t = slice(k * T, (k + 1) * T)
                nc.vector.tensor_tensor(x2lo[:, :, t], bank[k % 4][:, 0:D].rearrange("p (c t) -> p c t", c=NC),
                                        x2hi[:, :, t].bitcast(F32), ALU.subtract).then_inc(v_x2lo, 1)

            for k in range(B):
                wait(dve, pe_XT, k - 1)
                layernorm(1, xb_all[:, k * D:(k + 1) * D], k, x2n[k % 2][:], v_x2n)
                if k >= 1:
                    x2_low(k - 1)
            x2_low(B - 1)

            steps = [0]

            def step(ins):
                steps[0] += 1
                ins.then_inc(v_gate, 1)
                dve.wait_ge(v_gate, steps[0])

            def domains_in():
                dve.wait_ge(pe_td, 1)
                dve.wait_ge(arrived["b2"], 16)
                step(nc.vector.tensor_tensor(td[:], MB[0:B, 0:ND], b2_b[:], ALU.add))
                step(nc.vector.tensor_reduce(tdm[:], td[:], AX_X, ALU.max))
                step(nc.vector.tensor_scalar(td[:], td[:], tdm[:, 0:1], None, ALU.subtract))

            def domains_out():
                dve.wait_ge(a_td, 1)
                step(nc.vector.reciprocal(tdr[:], tds[:]))
                step(nc.vector.tensor_scalar(tdn[:], td[:], tdr[:, 0:1], 0.5, ALU.mult, ALU.mult))

            def domains_spread():
                dve.wait_ge(pe_tdT, 1)
                step(nc.vector.tensor_copy(tdT[:], MA[0:ND, 0:B]))
                step(nc.vector.tensor_copy(tdb[:].rearrange("p (b t) -> p b t", b=B),
                                           tdT[:].rearrange("p (b a) -> p b a", a=1).broadcast_to([ND, B, T])))

            def top_experts():
                dve.wait_ge(pe_logits, 1)
                dve.wait_ge(arrived["rbias"], 16)
                src = MB[:].rearrange("p (b e) -> p b e", b=B)
                dve.wait_ge(g_const, 5)
                nc.vector.tensor_copy(lg[:], src)
                step(nc.vector.tensor_tensor(lb[:, :, 0:E], src,
                                             rbias_b[:].rearrange("p (a e) -> p a e", a=1).broadcast_to([P, B, E]), ALU.add))
                step(nc.vector.tensor_reduce(lmax[:], lg[:], AX_X, ALU.max))
                step(nc.vector.tensor_tensor(ex[:], lg[:], lmax[:].rearrange("p (b a) -> p b a", a=1).broadcast_to([P, B, E]),
                                             ALU.subtract))
                for b in range(B):
                    ins = nc.vector.max(top[:, b, :], lb[:, b, 0:E])
                step(ins)
                step(nc.vector.memset(top[:, :, TOPK:8], FAR))
                for b in range(B):
                    ins = nc.vector.match_replace(rep[:, b, :], top[:, b, :], lb[:, b, :], -FAR)
                step(ins)
                step(nc.vector.tensor_tensor(sel[:], rep[:, :, 0:E], lb[:, :, 0:E], ALU.not_equal))

            def combine():
                dve.wait_ge(a_ex, 1)
                step(nc.vector.tensor_reduce(z_all[:], ex[:], AX_X, ALU.add))
                step(nc.vector.tensor_tensor(ex[:], ex[:], sel[:], ALU.mult))
                step(nc.vector.tensor_reduce(z_top[:], ex[:], AX_X, ALU.add))
                step(nc.vector.scalar_tensor_tensor(out=z_all[:], in0=z_all[:], scalar=GUARD, in1=z_top[:],
                                                    op0=ALU.mult, op1=ALU.add))
                step(nc.vector.reciprocal(z_top[:], z_all[:]))
                step(nc.vector.tensor_tensor(cw[:], ex[:], z_top[:].rearrange("p (b a) -> p b a", a=1).broadcast_to([P, B, E]),
                                             ALU.mult))

            def combine_by_expert():
                for i, m in enumerate((MA, MB)):
                    dve.wait_ge(pe_cT, i + 1)
                    step(nc.vector.tensor_copy(cT[:, i * HALF:(i + 1) * HALF], m[0:E, :]))

            gate = {0: domains_in, 1: domains_out, 2: domains_spread, 3: top_experts, 4: combine, 6: combine_by_expert}

            def hidden(v, half, i, n_cb):
                dve.wait_ge(pe_U, v + 1)
                dve.wait_ge(a_sil, v + 1)
                if n_cb is None:
                    wait(dve, v_hlo, v - 1)
                    nc.vector.tensor_tensor(hh[half][:], U_ps[:], sil[half][:], ALU.mult).then_inc(v_su, 1)
                    dve.wait_ge(v_su, v + 1)
                    nc.vector.engine_nop().then_inc(v_h, 1)
                else:
                    nc.vector.tensor_tensor(su[half][:], U_ps[:], sil[half][:], ALU.mult).then_inc(v_su, 1)
                    dve.wait_ge(v_su, v + 1)
                    dve.wait_ge(cb_in[i], n_cb)
                    nc.vector.tensor_tensor(hh[half][:], su[half][:], cb[i][:, half * HALF:(half + 1) * HALF],
                                            ALU.mult).then_inc(v_h, 1)
                dve.wait_ge(a_hhi, v + 1)
                nc.vector.tensor_tensor(hlo[half][:], hh[half][:], hhi[half][:].bitcast(F32), ALU.subtract).then_inc(v_hlo, 1)

            for v in range(2 * SHARED_UNITS):
                if v in gate:
                    gate[v]()
                hidden(v, v % 2, 0, None)
            assert steps[0] == GATE_STEPS, steps
            with dve.Fori((SHARED_UNITS) // 2, (UNITS) // 2) as t:
                u = 2 * t
                for i in range(2):
                    for half in range(2):
                        hidden(2 * (u + i) + half, half, i, 16 * (u - SHARED_UNITS) + 32)
            dve.wait_ge(pe_D, 2 * UNITS)
            for half in range(2):
                nc.vector.tensor_copy(yT[:, 1, half * HALF:(half + 1) * HALF], ACC[half][1][:]).then_inc(v_yT, 1)
            for q in range(4):
                dve.wait_ge(pe_Y, q + 1)
                nc.vector.tensor_tensor(y[:, 2 * q * D:(2 * q + 2) * D], bank[q % 2][:],
                                        xb_all[:, 2 * q * D:(2 * q + 2) * D], ALU.add).then_inc(v_y, 1)

        @block.tensor
        def _(pe):
            mm = nc.tensor.matmul

            def turn(out_, in_):
                k = in_.shape[0]
                return nc.tensor.transpose(out_, in_, ident[0:k, 0:k])

            pe.wait_ge(arrived["ident"], 16)
            pe.wait_ge(arrived["wq"], 16)
            for c in range(NC):
                for a in range(NC):
                    last = turn(bank[0][:, (c * NC + a) * P:(c * NC + a + 1) * P], wq_n[:, a, c * P:(c + 1) * P])
            last.then_inc(pe_w, 1)
            pe.wait_ge(arrived["wfc"], 16)
            for c in range(NC):
                for a in range(NC):
                    last = turn(bank[1][:, (c * NC + a) * P:(c * NC + a + 1) * P], wfc_n[:, a, c * P:(c + 1) * P])
            last.then_inc(pe_w, 1)
            pe.wait_ge(arrived["wkv"], 32)
            pe.wait_ge(arrived["wr"], 16)
            for c in range(NC):
                turn(bank[2][:, c * P:(c + 1) * P], wkv_n[:, c * P:(c + 1) * P])
            for c in range(NC):
                last = turn(bank[2][:, NC * P + c * E:NC * P + (c + 1) * E], wr_n[:, c:D:NC])
            last.then_inc(pe_w, 1)
            for n_ in ("w1", "w2", "aff"):
                pe.wait_ge(arrived[n_], 16)
            for c in range(NC):
                turn(bank[3][:, c * P:(c + 1) * P], w1_n[:, c:D:NC])
            turn(bank[3][:, NC * P:NC * P + ND], w2_n[:])
            turn(bank[3][0:ND, NC * P + 64:NC * P + 64 + E], aff_n[:]).then_inc(pe_w, 1)
            pe.wait_ge(v_w, 1)
            pe.wait_ge(a_w, 1)
            pe.wait_ge(v_const, 1)

            def rows(s):
                return slice(s * STRIP, (s + 1) * STRIP)

            def body(n, odd, has):
                def scores_by_query(i):
                    k, G, o = n + 1, i // J, 1 - odd
                    if i == 0:
                        pe.wait_ge(a_kT, k + 1)
                        pe.wait_ge(a_qT, k + 1)
                    if i == 1:
                        wait(pe, v_D, k)
                    if i == J:
                        pe.wait_ge(v_qT, k + 1)
                    if i > 1:
                        pe.wait_ge(v_max, 8 * k + i - 1)
                    mm(S_ps[i % 2][:], qT[o][:, i * T:(i + 1) * T], kT[o][:, G * SG * T:(G + 1) * SG * T],
                       start=True, stop=True).then_inc(pe_S, 1)

                def scores_by_key(g):
                    G = g // SG
                    if g == 0:
                        pe.wait_ge(v_D, n + 1)
                    wait(pe, a_exp, 8 * n + g - 1)
                    mm(ST_ps[g % 2][:], kT[odd][:, g * T:(g + 1) * T], qT[odd][:, G * J * T:(G + 1) * J * T],
                       start=True, stop=False)
                    mm(ST_ps[g % 2][:], onesel[:, g * P:(g + 1) * P], Dm[:], start=False, stop=True).then_inc(pe_ST, 1)

                def values(k, par, G):
                    pe.wait_ge(g_V, k + 1)
                    pe.wait_ge(a_exp, 8 * k + SG * G + SG)
                    wait(pe, a_O, 2 * k - 1 + G)
                    for s in range(SG):
                        g = SG * G + s
                        last = mm(O_ps[G][rows(s), :], Vw[par][:, g * STRIP:(g + 1) * STRIP], Pr[g][:], start=True, stop=True)
                    last.then_inc(pe_PV, 1)

                def heads_by_query(k, G):
                    pe.wait_ge(a_O, 2 * k + G + 1)
                    for j in range(J):
                        last = turn((MA, MB)[G][:, j * P:(j + 1) * P], O_sb[G][:, j * T:(j + 1) * T])
                    last.then_inc(pe_OT, 1)

                def query_operand(k, G):
                    for j in range(J):
                        last = turn((MA, MB)[G][:, j * T:(j + 1) * T],
                                    qrep[:, (G * J + j) * P:(G * J + j + 1) * P].bitcast(F32))
                    last.then_inc(pe_QKT, 1)

                if has(n + 1):
                    k = n + 1
                    pe.wait_ge(v_lo, k + 1)
                    wait(pe, v_max, 8 * k - 1)
                    for G in range(NG):
                        last = turn(S_ps[0][:, G * T:(G + 1) * T], krep[:, G * P:(G + 1) * P].bitcast(F32))
                    last.then_inc(pe_QKT, 1)
                    query_operand(k, 0)
                if has(n - 1):
                    values(n - 1, 1 - odd, 1)
                for g in range(GROUPS):
                    if has(n):
                        scores_by_key(g)
                    if g == 0 and has(n + 1):
                        wait(pe, v_x2, n - 1)
                        query_operand(n + 1, 1)
                    if g == 1 and has(n - 1):
                        if has(n + 1):
                            pe.wait_ge(a_qT, n + 2)
                        heads_by_query(n - 1, 0)
                    if g == 2 and has(n - 1):
                        if has(n + 1):
                            pe.wait_ge(v_qT, n + 2)
                        else:
                            pe.wait_ge(v_x2, n - 1)
                        heads_by_query(n - 1, 1)
                    if g == 3 and has(n + 2):
                        k = n + 2
                        pe.wait_ge(ctx_arrived[odd], 8 * (k - odd) + 16)
                        if has(n - 1):
                            pe.wait_ge(v_norm, 2 * n)
                        elif has(n + 1):
                            pe.wait_ge(v_qT, n + 2)
                        pe.wait_ge(v_xn, k + 1)
                        for c in range(NC):
                            turn(MB[:, c * T:(c + 1) * T], xn[:, c * P:(c + 1) * P])
                        for c in range(NC):
                            last = turn(MB[:, D + c * T:D + (c + 1) * T], ctx_in[odd][:, c * P:(c + 1) * P])
                        last.then_inc(pe_T1, 1)
                    if g == 4 and has(n - 1):
                        pe.wait_ge(v_norm, 2 * n)
                        if has(n + 2):
                            pe.wait_ge(a_xcT, n + 3)
                        for c in range(NC):
                            last = turn(MB[:, c * T:(c + 1) * T], attn[:, c * P:(c + 1) * P])
                        last.then_inc(pe_AT, 1)
                    if g == 5 and has(n + 2):
                        k = n + 2
                        pe.wait_ge(a_xcT, k + 1)
                        if has(n - 1):
                            pe.wait_ge(v_norm, 2 * (n - 1) + 1)
                        elif has(n + 1):
                            pe.wait_ge(a_qT, n + 2)
                        for c in range(NC):
                            mm(MA[:, 0:D], xcT[:, c * T:(c + 1) * T], wqT[:, c * D:(c + 1) * D], start=(c == 0), stop=(c == NC - 1))
                        for c in range(NC):
                            last = mm(MA[:, D:D + P], xcT[:, D + c * T:D + (c + 1) * T], wkvT[:, c * P:(c + 1) * P],
                                      start=(c == 0), stop=(c == NC - 1))
                        last.then_inc(pe_PJ, 1)
                    if g == 5 and has(n):
                        values(n, odd, 0)
                    if g == 7 and has(n - 1):
                        pe.wait_ge(a_attnT, n)
                        for c in range(NC):
                            last = mm(MB[:, 0:D], attnT[:, c * T:(c + 1) * T], wfcT[:, c * D:(c + 1) * D],
                                      start=(c == 0), stop=(c == NC - 1))
                        last.then_inc(pe_FC, 1)
                    if has(n + 1):
                        for i in SCORES_AT[g]:
                            scores_by_query(i)
                if has(n + 1):
                    k = n + 1
                    pe.wait_ge(v_ml, k + 1)
                    if isinstance(k, int) and k == 0:
                        pe.wait_ge(g_const, 3)
                    turn(S_ps[1][:, 0:T], ml[:].rearrange("p z h a -> p (z h a)").bitcast(F32)).then_inc(pe_MT, 1)

            iterations(pe, body)

            for k in range(B):
                m = bank[k % 4]
                pe.wait_ge(v_x2n, k + 1)
                pe.wait_ge(g_const, 4)
                wait(pe, v_x2lo, k - 3)
                for c in range(NC):
                    turn(m[:, c * T:(c + 1) * T], x2n[k % 2][:, c:D:NC])
                for c in range(NC):
                    last = mm(m[:, D + c:D + c + 1], x2n[k % 2][:, c:D:NC], inv_t[:, 0:1], start=True, stop=True)
                last.then_inc(pe_XT, 1)

            def domains_hidden():
                pe.wait_ge(v_x2lo, B)
                pe.wait_ge(v_w, 5)
                for c in range(NC):
                    last = mm(MA[:, 0:B], w1T[:, c * P:(c + 1) * P], xmT[:, c, :], start=(c == 0), stop=(c == NC - 1))
                last.then_inc(pe_h1, 1)

            def domains_logits():
                pe.wait_ge(a_h1, 1)
                mm(MB[0:B, 0:ND], h1T[:], w2T[:], start=True, stop=True).then_inc(pe_td, 1)

            def domains_turn():
                pe.wait_ge(v_gate, 5)
                turn(MA[0:ND, 0:B], tdn[:]).then_inc(pe_tdT, 1)

            def logits():
                pe.wait_ge(v_gate, 7)
                for b in range(B):
                    o = MB[:, b * E:(b + 1) * E]
                    t = slice(b * T, (b + 1) * T)
                    parts = [(c, xs, ws) for c in range(NC) for xs in (x2hi, x2lo) for ws in (wrT_hi, wrT_lo)]
                    for i, (c, xs, ws) in enumerate(parts):
                        mm(o, xs[:, c, t], ws[:, c * E:(c + 1) * E], start=(i == 0), stop=False)
                    last = mm(o, tdb[:, t], affT[:], start=False, stop=True)
                last.then_inc(pe_logits, 1)

            def combine_turn():
                pe.wait_ge(v_gate, GATE_CW)
                for b in range(B):
                    m = (MA, MB)[b // (B // 2)]
                    last = turn(m[0:E, (b % (B // 2)) * T:(b % (B // 2) + 1) * T], cw[:, b, :])
                    if b % (B // 2) == B // 2 - 1:
                        last.then_inc(pe_cT, 1)

            def product(out_, w_hi, w_lo, r_hi, r_lo, chunks, first, last_):
                n_ = 3 * len(chunks)
                i = 0
                for c in chunks:
                    for w, r in ((w_hi, r_hi), (w_hi, r_lo), (w_lo, r_hi)):
                        ins = mm(out_, w(c), r(c), start=(first and i == 0), stop=(last_ and i == n_ - 1))
                        i += 1
                return ins

            def gate_up(v, half, i):
                t = slice(half * HALF, (half + 1) * HALF)
                for m, (bank_, free, done) in enumerate(((G_ps, a_sil, pe_G), (U_ps, v_su, pe_U))):
                    wait(pe, free, v)
                    product(bank_[:], lambda c: whi[i][:, m * D + c * P:m * D + (c + 1) * P],
                            lambda c: wlo[i][:, m * D + c * P:m * D + (c + 1) * P],
                            lambda c: x2hi[:, c, t], lambda c: x2lo[:, c, t], range(NC), True, True).then_inc(done, 1)

            def down(v, half, i, first=False, last_=False):
                pe.wait_ge(v_hlo, v + 1)
                for dh in range(NC):
                    ins = product(ACC[half][dh][:], lambda c: whi[i][:, 2 * D + dh * P:2 * D + (dh + 1) * P],
                                  lambda c: wlo[i][:, 2 * D + dh * P:2 * D + (dh + 1) * P],
                                  lambda c: hhi[half][:], lambda c: hlo[half][:], range(1), first, last_)
                ins.then_inc(pe_D, 1)

            domains_hidden()
            gate = {0: domains_logits, 1: domains_turn, 2: logits, 5: combine_turn}
            for v in range(2 * SHARED_UNITS):
                u, half = divmod(v, 2)
                if half == 0:
                    pe.wait_ge(g_wlo, u + 1)
                gate_up(v, half, u % 2)
                if v >= 1:
                    down(v - 1, 1 - half, (v - 1) // 2 % 2, first=(v - 1 < 2))
                if v in gate:
                    gate[v]()
            def two_units(u, final=False):
                for i in range(2):
                    pe.wait_ge(g_wlo, u + i + 1)
                    for half in range(2):
                        v = 2 * (u + i) + half
                        gate_up(v, half, i)
                        down(v - 1, 1 - half, i if half else 1 - i, last_=(final and i == 1 and half == 1))

            with pe.Fori(SHARED_UNITS // 2, UNITS // 2 - 1) as t:
                two_units(2 * t)
            two_units(UNITS - 2, final=True)
            down(2 * UNITS - 1, 1, 1, last_=True)
            pe.wait_ge(a_yT, 2)
            pe.wait_ge(v_yT, 2)
            for q in range(4):
                if q >= 2:
                    pe.wait_ge(v_y, q - 1)
                for b in (2 * q, 2 * q + 1):
                    for dh in range(NC):
                        last = turn(bank[q % 2][:, (b % 2) * D + dh * P:(b % 2) * D + (dh + 1) * P],
                                    yT[:, dh, b * T:(b + 1) * T])
                last.then_inc(pe_Y, 1)


GATE_EX = 10
GATE_CW = 20
GATE_STEPS = 22

_INS = ["x", "ctx_2048", "L0_xattn_Wq", "L0_xattn_Wk", "L0_xattn_Wv", "L0_xattn_Wfc", "L0_xattn_bfc", "L0_ffn_Wr",
        "L0_ffn_router_bias", "L0_ffn_affinity", "L0_ffn_te_W1", "L0_ffn_te_b1", "L0_ffn_te_W2", "L0_ffn_te_b2",
        "L0_ffn_Wg", "L0_ffn_Wu", "L0_ffn_Wd", "L0_ffn_Sg", "L0_ffn_Su", "L0_ffn_Sd"]


def kernel(**inputs):
    import numpy as _np
    import concourse.bacc as _bacc
    from concourse import mybir as _mybir
    from concourse.bass_utils import run_bass_kernel_spmd as _run

    nc = _bacc.Bacc("TRN2", target_bir_lowering=False, num_devices=1)
    arrays = {f"in_{n}": _np.ascontiguousarray(inputs[n]) for n in _INS}
    rows = _np.arange(2 * HEADS)
    group = rows // (2 * SG * J) * SG + rows // 2 % SG
    arrays["const_ident"] = _np.eye(P, dtype=_np.float32)
    arrays["const_onesel"] = _np.repeat((group[:, None] == _np.arange(GROUPS)[None]).astype(_np.float32), P, axis=1)
    arrays["const_jmask"] = (rows[:, None] // (2 * SG) % J == _np.arange(J)[None]).astype(_np.float32)
    args = [nc.dram_tensor(n, a.shape, _mybir.dt.from_np(a.dtype), kind="ExternalInput").ap() for n, a in arrays.items()]
    out = nc.dram_tensor("out_0", (B, T, D), _mybir.dt.float32, kind="ExternalOutput").ap()
    build(nc, *args, out)
    result = _run(nc, [arrays], core_ids=[0])
    return result.results[0]["out_0"]
```

```python
from contextlib import ExitStack

import concourse.bass as bass
from concourse import mybir

F32 = mybir.dt.float32
F32R = mybir.dt.float32r
I32 = mybir.dt.int32
ACT = mybir.ActivationFunctionType
ALU = mybir.AluOpType
AX_X = mybir.AxisListType.X

P = 128
B, T, D = 8, 128, 256
NC = D // P
HEADS, GROUPS = 32, 8
J = HEADS // GROUPS
HD = D // HEADS
STRIP = 32
SG = P // STRIP
NG = GROUPS // SG
E, F = 64, 64
TOPK = 4
H_SHARED = 256
N_SHARED = 2
ND = 4
TOK = B * T
HALF = TOK // 2
SHARED_UNITS = N_SHARED * H_SHARED // P
EXPERT_UNITS = E * F // P
UNITS = SHARED_UNITS + EXPERT_UNITS
SHARED_STEPS = 2 * SHARED_UNITS
EARLY = 3
EPS = 1e-5
SCALE = float(HD) ** -0.5
GUARD = 1e-8
FAR = 3.0e38


GATE = ("logits without the domains' share", "domain logits", "their maximum", "domain logits less their maximum",
        "one over the domains' sum", "half the domain shares", "shares by domain", "shares for every token",
        "logits", "largest logit", "its negative", "logits with bias", "eight largest",
        "four largest and fillers", "four largest struck out", "chosen", "exp of the chosen",
        "their sum", "guarded sum", "one over it", "combine weights", "combine weights by expert")
LN_STEPS = 7


def gate_step(name):
    return GATE.index(name) + 1


def build(nc, x, ctx, Wq, Wk, Wv, Wfc, bfc, Wr, rbias, aff, W1, b1, W2, b2, Wg, Wu, Wd, Sg, Su, Sd,
          ident_d, onesel_d, jmask_d, out):
    c_dram = nc.dram_tensor("combine_scratch", (E, TOK), F32, kind="Internal").ap()
    with ExitStack() as stack:
        def sb(name, shape, dt=F32):
            return stack.enter_context(nc.sbuf_tensor(name, shape, dt))

        def sem(name):
            return stack.enter_context(nc.semaphore(name))

        bank = [stack.enter_context(nc.psum_tensor(f"bank{i}", [P, 512], F32)) for i in range(8)]
        S_ps, ST_ps, O_ps, MA, MB = bank[0:2], bank[2:4], bank[4:6], bank[6], bank[7]
        G_ps, U_ps = bank[0], bank[1]
        ACC = [bank[2:4], bank[4:6]]

        ident = sb("ident", [P, P])
        onesel_raw = sb("onesel_raw", [2 * HEADS, GROUPS * P])
        onesel = sb("onesel", [2 * HEADS, GROUPS * P], F32R)
        jmask = sb("jmask", [2 * HEADS, J])
        inv_t = sb("inv_t", [P, 2])
        wq_n = sb("wq_n", [P, NC, D])
        wfc_n = sb("wfc_n", [P, NC, D])
        wkv_n = sb("wkv_n", [P, D])
        wr_n = sb("wr_n", [E, D])
        w1_n = sb("w1_n", [P, D])
        w2_n = sb("w2_n", [ND, P])
        aff_n = sb("aff_n", [E, ND])
        wqT = sb("wqT", [P, NC * D])
        wfcT = sb("wfcT", [P, NC * D])
        wkvT = sb("wkvT", [P, NC * P])
        wrT = sb("wrT", [P, NC * E])
        wrT_hl = sb("wrT_hl", [P, NC, 2, E], F32R)
        w1T = sb("w1T", [P, NC * P])
        w2T = sb("w2T", [P, ND])
        affT = sb("affT", [ND, E])
        bfc_b = sb("bfc_b", [P, D])
        b1_c = sb("b1_c", [P, 1])
        b2_b = sb("b2_b", [B, ND])
        rbias_b = sb("rbias_b", [P, E])

        x_all = sb("x_all", [P, B * D])
        ctx_in = [sb(f"ctx_in{i}", [P, D]) for i in range(2)]
        xb_all = sb("xb_all", [P, B * D])
        stats = sb("stats", [P, 2, 2, 3])
        terms = sb("terms", [P, 2, 3])
        moments = sb("moments", [P, 2, 3])
        moment_of = sb("moment_of", [P, 2, 3])
        apart = sb("apart", [P, 2])
        var = sb("var", [P, 2])
        eps = sb("eps", [P, 2])
        minus_half = sb("minus_half", [P, 2])
        rstd = sb("rstd", [P, 2])
        xn = sb("xn", [P, D])
        xcT = sb("xcT", [P, 2 * D])
        qrep = sb("qrep", [P, HEADS * STRIP], F32R)
        krep = sb("krep", [P, GROUPS * STRIP], F32R)
        qT = [sb(f"qT{i}", [P, NG * J * T], F32R) for i in range(2)]
        kT = [sb(f"kT{i}", [P, NG * SG * T], F32R) for i in range(2)]
        Vw = [sb(f"Vw{i}", [P, GROUPS * STRIP]) for i in range(2)]
        v_sb = sb("v_sb", [P, GROUPS * HD])
        mx = [sb(f"mx{i}", [P, HEADS]) for i in range(2)]
        ml = sb("ml", [P, 2, HEADS, 2], F32R)
        Dm = sb("Dm", [2 * HEADS, J * T], F32R)
        Pr_all = sb("Pr_all", [P, GROUPS * J * T])
        Pr = [Pr_all[:, g * J * T:(g + 1) * J * T] for g in range(GROUPS)]
        O_sb = [sb(f"O_sb{i}", [P, J * T]) for i in range(NG)]
        rec = sb("rec", [P, NG, J * SG])
        attn = sb("attn", [P, D])
        attnT = sb("attnT", [P, D])
        x2n = sb("x2n", [P, D])
        x2hi = sb("x2hi", [P, NC, TOK], F32R)
        x2lo = sb("x2lo", [P, NC, TOK], F32R)
        xmT = sb("xmT", [P, NC, B])

        h1T = sb("h1T", [P, B])
        td = sb("td", [B, ND])
        tdm = sb("tdm", [B, 1])
        tds = sb("tds", [B, 1])
        tdr = sb("tdr", [B, 1])
        tdn = sb("tdn", [B, ND])
        tdT = sb("tdT", [ND, B])
        tdb = sb("tdb", [ND, B * T])
        lg_hi = sb("lg_hi", [P, B, E])
        lg = sb("lg", [P, B, E])
        lb = sb("lb", [P, B, E + 8])
        top = sb("top", [P, B, 8])
        rep = sb("rep", [P, B, E + 8])
        sel = sb("sel", [P, B, E])
        lmax = sb("lmax", [P, B])
        minus_lmax = sb("minus_lmax", [P, B])
        ex = sb("ex", [P, B, E])
        z_all = sb("z_all", [P, B])
        z_top = sb("z_top", [P, B])
        cw = sb("cw", [P, B, E])
        cT = sb("cT", [E, TOK])

        raw = [sb(f"raw{i}", [P, 3 * D]) for i in range(2)]
        whi = [sb(f"whi{i}", [P, 3 * D], F32R) for i in range(SHARED_UNITS)]
        wlo = [sb(f"wlo{i}", [P, 3 * D], F32R) for i in range(SHARED_UNITS)]
        cb = [sb(f"cb{i}", [P, TOK]) for i in range(2)]
        sil = [sb(f"sil{i}", [P, HALF]) for i in range(2)]
        su = [sb(f"su{i}", [P, HALF]) for i in range(2)]
        hh = [sb(f"hh{i}", [P, HALF]) for i in range(2)]
        hhi = [sb(f"hhi{i}", [P, HALF], F32R) for i in range(2)]
        hlo = [sb(f"hlo{i}", [P, HALF], F32R) for i in range(2)]
        yT = Pr_all[:, 0:NC * TOK].rearrange("p (c t) -> p c t", c=NC)
        y = x_all

        NW = ["ident", "wq", "wkv", "onesel", "jmask", "wfc", "wr", "w1", "w2", "aff", "bfc", "b1", "b2", "rbias"]
        arrived = {n: sem(f"arrived_{n}") for n in NW}
        x_first, x_rest = sem("x_first"), sem("x_rest")
        ctx_arrived = [sem(f"ctx_arrived{i}") for i in range(2)]
        raw_in = [sem(f"raw_in{i}") for i in range(2)]
        cb_in = [sem(f"cb_in{i}") for i in range(2)]
        c_out = sem("c_out")
        y_out = sem("y_out")
        pe_w = sem("pe_w")
        pe_T1, pe_PJ, pe_QKT, pe_S, pe_MT, pe_ST, pe_PV, pe_OT, pe_AT, pe_FC, pe_XT = (
            sem(f"pe_{n}") for n in ("T1", "PJ", "QKT", "S", "MT", "ST", "PV", "OT", "AT", "FC", "XT"))
        pe_lg, pe_h1, pe_td, pe_tdT, pe_dom, pe_cT = (sem(f"pe_{n}") for n in ("lg", "h1", "td", "tdT", "dom", "cT"))
        pe_G, pe_U, pe_D, pe_Y = (sem(f"pe_{n}") for n in ("G", "U", "D", "Y"))
        a_w, a_xcT, a_qkv, a_V, a_kT, a_qT, a_exp, a_O, a_attnT, a_x2hi = (
            sem(f"a_{n}") for n in ("w", "xcT", "qkv", "V", "kT", "qT", "exp", "O", "attnT", "x2hi"))
        a_lg, a_h1, a_td, a_ex, a_sil, a_hhi, a_whi, a_yT = (sem(f"a_{n}") for n in ("lg", "h1", "td", "ex", "sil", "hhi", "whi", "yT"))
        (v_w, v_const, v_stats, v_xn, v_lo, v_qT, v_max, v_mhi, v_ml, v_D, v_rec, v_norm, v_x2, v_x2n, v_x2lo) = (
            sem(f"v_{n}") for n in ("w", "const", "stats", "xn", "lo", "qT", "max", "mhi", "ml", "D", "rec", "norm",
                                    "x2", "x2n", "x2lo"))
        v_gate, v_su, v_h, v_hlo, v_yT, v_y = (sem(f"v_{n}") for n in ("gate", "su", "h", "hlo", "yT", "y"))
        g_const, g_zero, g_xb, g_ln, g_wlo = (sem(f"g_{n}") for n in ("const", "zero", "xb", "ln", "wlo"))

        FIRST_N, LAST_N = -2, B + 1
        LOOP = (2, 6)

        def iterations(eng, body):
            def has(k):
                return 0 <= k < B
            for n in range(FIRST_N, LOOP[0]):
                body(n, n % 2, has)
            with eng.Fori(LOOP[0] // 2, LOOP[1] // 2) as t:
                n = 2 * t
                body(n, 0, lambda k: True)
                body(n + 1, 1, lambda k: True)
            for n in range(LOOP[1], LAST_N + 1):
                body(n, n % 2, has)

        SPLIT_AT = {-1: (0, 1), 0: (2,), 1: (3,)}

        SCORES_AT = ((), (0,), (1, 2), (3,), (4, 5), (6,), (7,), ())

        def n_is(n, value):
            return isinstance(n, int) and n == value

        def wait(eng, s, value):
            if isinstance(value, int) and value <= 0:
                return
            eng.wait_ge(s, value)

        block = stack.enter_context(nc.Block())

        @block.sync
        def _(sp):
            sp.dma_start(x_all[:, 0:D], x[0]).then_inc(x_first, 16)
            sp.dma_start(ident[:], ident_d).then_inc(arrived["ident"], 16)
            sp.dma_start(ctx_in[0][:], ctx[0]).then_inc(ctx_arrived[0], 16)
            sp.dma_start(wq_n[:], Wq.rearrange("(a p) i -> p a i", p=P)).then_inc(arrived["wq"], 16)
            sp.dma_start(wkv_n[0:64, :], Wk).then_inc(arrived["wkv"], 16)
            sp.dma_start(wkv_n[64:128, :], Wv).then_inc(arrived["wkv"], 16)
            sp.dma_start(x_all[:, D:].rearrange("p (b d) -> p b d", b=B - 1),
                         x[1:B].rearrange("b p d -> p b d")).then_inc(x_rest, 16)
            sp.dma_start(ctx_in[1][:], ctx[1]).then_inc(ctx_arrived[1], 16)
            sp.dma_start(onesel_raw[:], onesel_d).then_inc(arrived["onesel"], 16)
            sp.dma_start(jmask[:], jmask_d).then_inc(arrived["jmask"], 16)
            sp.dma_start(wfc_n[:], Wfc.rearrange("(a p) i -> p a i", p=P)).then_inc(arrived["wfc"], 16)
            sp.dma_start(wr_n[:], Wr).then_inc(arrived["wr"], 16)
            sp.dma_start(w1_n[:], W1).then_inc(arrived["w1"], 16)
            sp.dma_start(w2_n[:], W2).then_inc(arrived["w2"], 16)
            sp.dma_start(aff_n[:], aff).then_inc(arrived["aff"], 16)
            sp.dma_start(bfc_b[:], bfc.rearrange("(a n) -> a n", a=1).broadcast_to([P, D])).then_inc(arrived["bfc"], 16)
            sp.dma_start(b1_c[:], b1.rearrange("(p a) -> p a", a=1)).then_inc(arrived["b1"], 16)
            sp.dma_start(b2_b[:], b2.rearrange("(a n) -> a n", a=1).broadcast_to([B, ND])).then_inc(arrived["b2"], 16)
            sp.dma_start(rbias_b[:], rbias.rearrange("(a n) -> a n", a=1).broadcast_to([P, E])).then_inc(arrived["rbias"], 16)

            def load_unit(i, gate_up, down):
                for m in range(2):
                    dst = raw[i][:, m * D:(m + 1) * D]
                    src = gate_up[m]
                    if len(src.shape) == 4:
                        sp.dma_start(dst.rearrange("p (e c f) -> p e c f", e=2, c=NC), src).then_inc(raw_in[i], 16)
                    else:
                        sp.dma_start(dst.rearrange("p (c f) -> p c f", c=NC), src).then_inc(raw_in[i], 16)
                sp.dma_start(raw[i][:, 2 * D:3 * D], down).then_inc(raw_in[i], 16)

            def shared(u):
                s, h = divmod(u, H_SHARED // P)
                cols = slice(h * P, (h + 1) * P)
                return ([w[s, :, cols].rearrange("(p c) f -> p c f", c=NC) for w in (Sg, Su)],
                        Sd[s, h * P:(h + 1) * P, :])

            def experts(u):
                e = 2 * (u - SHARED_UNITS)
                return ([w[bass.ds(e, 2)].rearrange("e (p c) f -> p e c f", c=NC) for w in (Wg, Wu)],
                        Wd.rearrange("e f d -> (e f) d")[bass.ds(e * F, P), :])

            def load_combine(i, u):
                e = 2 * (u - SHARED_UNITS)
                for k in range(2):
                    sp.dma_start(cb[i][k * F:(k + 1) * F, :],
                                 c_dram[bass.ds(e + k, 1), :].broadcast_to([F, TOK])).then_inc(cb_in[i], 16)

            for u in range(2):
                load_unit(u, *shared(u))

            def load_ctx(t):
                for i in range(2):
                    sp.wait_ge(pe_T1, 2 * t + i - 1)
                    sp.dma_start(ctx_in[i][:], ctx.rearrange("b p d -> (b p) d")[bass.ds((2 * t + i) * P, P), :])\
                      .then_inc(ctx_arrived[i], 16)

            load_ctx(1)
            for u in range(2, SHARED_UNITS):
                sp.wait_ge(g_wlo, u - 1)
                load_unit(u % 2, *shared(u))
            with sp.Fori(2, B // 2) as t:
                load_ctx(t)
            for u in range(SHARED_UNITS, SHARED_UNITS + 2):
                wait(sp, g_wlo, u - 1)
                load_unit(u % 2, *experts(u))
            sp.wait_ge(v_gate, gate_step("combine weights by expert"))
            sp.dma_start(c_dram, cT[:]).then_inc(c_out, 16)
            sp.wait_ge(c_out, 16)
            for u in range(SHARED_UNITS, SHARED_UNITS + 2):
                load_combine(u % 2, u)
            with sp.Fori((SHARED_UNITS + 2) // 2, (UNITS) // 2) as t:
                u = 2 * t
                for i in range(2):
                    sp.wait_ge(g_wlo, u + i - 1)
                    load_unit(i, *experts(u + i))
                    sp.wait_ge(v_h, 2 * (u + i) - 2)
                    load_combine(i, u + i)
            for q in range(4):
                sp.wait_ge(v_y, q + 1)
                sp.dma_start(out[2 * q:2 * q + 2].rearrange("b p d -> p b d"),
                             y[:, 2 * q * D:(2 * q + 2) * D].rearrange("p (b d) -> p b d", b=2)).then_inc(y_out, 16)
            sp.wait_ge(y_out, 64)

        @block.gpsimd
        def _(pool):
            for i in range(2):
                nc.gpsimd.memset(Vw[i][:], 1.0).then_inc(g_const, 1)
            for i in range(2):
                nc.gpsimd.memset(kT[i][:].bitcast(F32), 0.0).then_inc(g_zero, 1)
            nc.gpsimd.memset(ml[:, 1].bitcast(F32), 0.0).then_inc(g_const, 1)
            nc.gpsimd.memset(inv_t[:], 1.0 / T).then_inc(g_const, 1)
            nc.gpsimd.memset(lb[:, :, E:E + 8], FAR).then_inc(g_const, 1)
            for tile, value in ((moment_of[:, :, 0], 0.5), (moment_of[:, :, 1], 1.0 / D), (moment_of[:, :, 2], 0.25),
                                (eps[:], EPS), (minus_half[:], -0.5)):
                last = nc.gpsimd.memset(tile, value)
            last.then_inc(g_const, 1)

            add, sub, mul = ALU.add, ALU.subtract, ALU.mult

            def deviations(n, odd, has):
                done = [LN_STEPS * (n - FIRST_N)]

                def step(out_, a, b, op):
                    ins = nc.gpsimd.tensor_tensor(out_, a, b, op).then_inc(g_ln, 1)
                    done[0] = done[0] + 1
                    pool.wait_ge(g_ln, done[0])
                    return ins

                if has(n + 2) or has(n - 2):
                    pool.wait_ge(v_stats, n + 3)
                    if has(n + 1):
                        wait(pool, v_xn, n + 2)
                    if has(n - 3):
                        wait(pool, v_x2n, n - 2)
                step(terms[:, :, 0:2], stats[:, :, 0, 1:3], stats[:, :, 1, 1:3], add)
                step(apart[:], stats[:, :, 0, 1], stats[:, :, 1, 1], sub)
                step(terms[:, :, 2], apart[:], apart[:], mul)
                step(moments[:], terms[:], moment_of[:], mul)
                step(var[:], moments[:, :, 1], moments[:, :, 2], add)
                step(var[:], var[:], eps[:], add)
                step(rstd[:], var[:], minus_half[:], ALU.pow)

            pool.wait_ge(g_const, 6)
            pool.wait_ge(v_const, 1)

            def split(i, w, u, n_raw, used, pairs):
                pool.wait_ge(raw_in[i], n_raw)
                pool.wait_ge(a_whi, 2 * u + 1)
                wait(pool, pe_U, used)
                gu_lo = wlo[w][:, 0:2 * D]
                gu_hi = whi[w][:, 0:2 * D].bitcast(F32)
                gu = raw[i][:, 0:2 * D]
                if pairs:
                    for m in range(2):
                        s = slice(m * D, (m + 1) * D)
                        order = "p (e c f) -> p c e f"
                        nc.gpsimd.tensor_tensor(wlo[w][:, s].rearrange("p (c e f) -> p c e f", c=NC, e=2),
                                                raw[i][:, s].rearrange(order, c=NC, e=2),
                                                whi[w][:, s].bitcast(F32).rearrange("p (c e f) -> p c e f", c=NC, e=2),
                                                ALU.subtract)
                else:
                    nc.gpsimd.tensor_tensor(gu_lo, gu, gu_hi, ALU.subtract)
                pool.wait_ge(a_whi, 2 * u + 2)
                wait(pool, pe_D, used)
                nc.gpsimd.tensor_tensor(wlo[w][:, 2 * D:3 * D], raw[i][:, 2 * D:3 * D],
                                        whi[w][:, 2 * D:3 * D].bitcast(F32), ALU.subtract).then_inc(g_wlo, 1)

            def body(n, odd, has):
                deviations(n, odd, has)
                if n_is(n, 0):
                    pool.wait_ge(x_rest, 16)
                    pool.wait_ge(arrived["bfc"], 16)
                    for b in range(B):
                        nc.gpsimd.tensor_tensor(xb_all[:, b * D:(b + 1) * D], x_all[:, b * D:(b + 1) * D], bfc_b[:],
                                                ALU.add).then_inc(g_xb, 1)
                if isinstance(n, int) and n in SPLIT_AT:
                    for u in SPLIT_AT[n]:
                        split(u % 2, u, u, 48 * (u // 2 + 1), 0, False)

            iterations(pool, body)

            for i in range(2):
                split(i, i, SHARED_UNITS + i, 24 * SHARED_UNITS + 48, SHARED_UNITS + i + 1, True)
            with pool.Fori((SHARED_UNITS + 2) // 2, (UNITS) // 2) as t:
                u = 2 * t
                for i in range(2):
                    split(i, i, u + i, 24 * u + 48, 2 * (u + i) - 2, True)

        @block.scalar
        def _(act):
            copy, exp = ACT.Copy, ACT.Exp
            act.wait_ge(pe_w, 2)
            nc.scalar.activation(wkvT[:], bank[1][:, 0:NC * P], copy).then_inc(a_w, 1)

            def weights_hi(i, w, n_raw, used, pairs):
                act.wait_ge(raw_in[i], n_raw)
                wait(act, pe_U, used)
                for m in range(2):
                    s = slice(m * D, (m + 1) * D)
                    if pairs:
                        ins = nc.scalar.activation(whi[w][:, s].rearrange("p (c e f) -> p c e f", c=NC, e=2),
                                                   raw[i][:, s].rearrange("p (e c f) -> p c e f", c=NC, e=2), copy)
                    else:
                        ins = nc.scalar.activation(whi[w][:, s], raw[i][:, s], copy)
                ins.then_inc(a_whi, 1)
                wait(act, pe_D, used)
                nc.scalar.activation(whi[w][:, 2 * D:], raw[i][:, 2 * D:], copy).then_inc(a_whi, 1)

            def silu(v, i):
                act.wait_ge(pe_G, v + 1)
                wait(act, v_su, v - 1)
                nc.scalar.activation(sil[i][:], G_ps[:], ACT.Silu).then_inc(a_sil, 1)

            def hidden_hi(v, i):
                act.wait_ge(v_h, v + 1)
                wait(act, pe_D, v - 1)
                nc.scalar.activation(hhi[i][:], hh[i][:], copy).then_inc(a_hhi, 1)

            def body(n, odd, has):
                if has(n + 1):
                    k = n + 1
                    act.wait_ge(pe_QKT, 3 * k + 1)
                    wait(act, pe_ST, 8 * k - 8)
                    if isinstance(k, int) and k < 2:
                        act.wait_ge(g_zero, k + 1)
                    for s in range(SG):
                        last = nc.scalar.activation(
                            kT[1 - odd][s * STRIP:(s + 1) * STRIP, :].rearrange("p (G s t) -> p G s t", G=NG, s=SG)[:, :, s, :],
                            S_ps[0][s * STRIP:(s + 1) * STRIP, 0:NG * T].rearrange("p (G t) -> p G t", G=NG), copy)
                    last.then_inc(a_kT, 1)
                    act.wait_ge(pe_QKT, 3 * k + 2)
                    nc.scalar.activation(qT[1 - odd][:, 0:J * T], MA[:], copy).then_inc(a_qT, 1)
                for g in range(GROUPS):
                    if has(n):
                        act.wait_ge(pe_ST, 8 * n + g + 1)
                        wait(act, pe_PV, 2 * n - 1 + g // SG)
                        nc.scalar.activation(Pr[g], ST_ps[g % 2][:], exp, scale=SCALE).then_inc(a_exp, 1)
                    if isinstance(n, int) and n in SPLIT_AT and g == (2 if n < 0 else 7):
                        for u in SPLIT_AT[n]:
                            weights_hi(u % 2, u, 48 * (u // 2 + 1), 0, False)
                    if g == 4 and n_is(n, -1):
                        act.wait_ge(pe_w, 3)
                        nc.scalar.activation(wfcT[:], bank[4][:], copy).then_inc(a_w, 1)
                    if g == 0 and has(n - 1):
                        evac_O(n - 1, 1)
                    if g == 3 and (n_is(n, B) or n_is(n, B + 1)):
                        silu(n - B, (n - B) % 2)
                        hidden_hi(n - B, (n - B) % 2)
                    if g == 0 and has(n + 1):
                        k = n + 1
                        if isinstance(k, int) and k < 2:
                            act.wait_ge(g_const, 2)
                        act.wait_ge(a_qkv, k + 1)
                        nc.scalar.activation(Vw[1 - odd][:].rearrange("p (g r) -> p g r", g=GROUPS)[:, :, 0:HD],
                                             v_sb[:].rearrange("p (g d) -> p g d", g=GROUPS), copy).then_inc(a_V, 1)
                    if g == 3 and has(n + 2):
                        k = n + 2
                        act.wait_ge(pe_T1, k + 1)
                        wait(act, pe_PJ, k)
                        nc.scalar.activation(xcT[:], MB[:], copy).then_inc(a_xcT, 1)
                    if g == 4 and has(n - 2):
                        k = n - 2
                        act.wait_ge(pe_XT, k + 1)
                        nc.scalar.activation(xmT[:, :, bass.ds(k, 1)], MA[:, D:D + NC].rearrange("p (c a) -> p c a", a=1), copy)
                        nc.scalar.activation(x2hi[:, :, bass.ds(k * T, T)], MA[:, 0:D].rearrange("p (c t) -> p c t", c=NC),
                                             copy).then_inc(a_x2hi, 1)
                    if g == 4 and has(n - 1):
                        act.wait_ge(pe_AT, n)
                        wait(act, pe_FC, n - 1)
                        nc.scalar.activation(attnT[:], MB[:, 0:D], copy).then_inc(a_attnT, 1)
                    if g == 5 and has(n + 2):
                        k = n + 2
                        act.wait_ge(pe_PJ, k + 1)
                        wait(act, pe_QKT, 3 * k)
                        wait(act, a_V, k)
                        nc.scalar.activation(v_sb[:], MA[:, D + 64:D + 128], copy)
                        kv = krep[:].rearrange("p (g r d) -> p g r d", g=GROUPS, r=4)
                        nc.scalar.activation(kv[:, :, 0:2, :],
                                             MA[:, D:D + 64].rearrange("p (g a d) -> p g a d", g=GROUPS, a=1)
                                             .broadcast_to([P, GROUPS, 2, HD]), copy)
                        qv = qrep[:].rearrange("p (h r d) -> p h r d", h=HEADS, r=4)
                        nc.scalar.activation(qv[:, :, 0:4:2, :],
                                             MA[:, 0:D].rearrange("p (h a d) -> p h a d", h=HEADS, a=1)
                                             .broadcast_to([P, HEADS, 2, HD]), copy).then_inc(a_qkv, 1)
                    if g == 6 and has(n):
                        evac_O(n, 0)

            def evac_O(k, G):
                act.wait_ge(pe_PV, 2 * k + G + 1)
                wait(act, pe_OT, 2 * k - 1 + G)
                nc.scalar.activation(O_sb[G][:], O_ps[G][:], copy).then_inc(a_O, 1)

            iterations(act, body)

            silu(2, 0)
            act.wait_ge(pe_h1, 1)
            act.wait_ge(arrived["b1"], 16)
            nc.scalar.activation(h1T[:], MA[:, 0:B], ACT.Gelu, bias=b1_c[:, 0:1]).then_inc(a_h1, 1)
            hidden_hi(2, 0)
            for i in range(2):
                act.wait_ge(pe_lg, i + 1)
                nc.scalar.activation(lg_hi[:, i * B // 2:(i + 1) * B // 2, :],
                                     ACC[1][i][:].rearrange("p (b m e) -> p b m e", b=B // 2, m=2)[:, :, 0, :], copy).then_inc(a_lg, 1)
            act.wait_ge(v_gate, gate_step("domain logits less their maximum"))
            nc.scalar.activation(td[:], td[:], exp, accum_out=tds[:, 0:1]).then_inc(a_td, 1)
            for v in range(EARLY, SHARED_STEPS):
                silu(v, v % 2)
                if v == 4:
                    act.wait_ge(v_gate, gate_step("its negative"))
                    for b in range(B):
                        ins = nc.scalar.activation(ex[:, b, :], lg[:, b, :], exp, bias=minus_lmax[:, b:b + 1],
                                                   accum_out=z_all[:, b:b + 1])
                    ins.then_inc(a_ex, 1)
                hidden_hi(v, v % 2)
                if v == SHARED_STEPS - 2:
                    weights_hi(0, 0, 24 * SHARED_UNITS + 48, SHARED_UNITS + 1, True)
            def two_units(u, used_second):
                for i in range(2):
                    for half in range(2):
                        v = 2 * (u + i) + half
                        silu(v, half)
                        if half == 0:
                            weights_hi(1 - i, 1 - i, 24 * (u + 2 * i) + 48, 2 * (u + i) if i else used_second, True)
                        hidden_hi(v, half)

            two_units(SHARED_UNITS, SHARED_UNITS + 2)
            with act.Fori((SHARED_UNITS + 2) // 2, (UNITS - 2) // 2) as t:
                two_units(2 * t, 4 * t)
            for u in range(UNITS - 2, UNITS):
                for half in range(2):
                    silu(2 * u + half, half)
                    if half == 0 and u + 1 < UNITS:
                        weights_hi(1, 1, 24 * (UNITS - 2) + 48, 2 * u, True)
                    hidden_hi(2 * u + half, half)
            act.wait_ge(pe_D, 2 * UNITS)
            for half in range(2):
                nc.scalar.activation(yT[:, 0, half * HALF:(half + 1) * HALF], ACC[half][0][:], copy).then_inc(a_yT, 1)

        @block.vector
        def _(dve):
            nc.vector.memset(stats[:], 1.0).then_inc(v_const, 1)
            dve.wait_ge(v_const, 1)


            def statistics(n, has):
                wait(dve, g_ln, LN_STEPS * (n - FIRST_N))
                for i, k, rows in ((0, n + 2, x_all), (1, n - 2, xb_all)):
                    if has(k):
                        dve.wait_ge(x_first if isinstance(k, int) and k == 0 else x_rest, 16)
                        if i == 1:
                            dve.wait_ge(v_x2, k + 1)
                        last = nc.vector.bn_stats(stats[:, i].rearrange("p a s -> p (a s)"), rows[:, bass.ds(k * D, D)])
                last.then_inc(v_stats, 1)

            def query_weights():
                dve.wait_ge(pe_w, 1)
                for cG in range(NC * NG):
                    last = nc.vector.tensor_copy(wqT[:, cG * P:(cG + 1) * P].rearrange("p (j s d) -> p j s d", j=J, s=SG),
                                                 bank[0][:, cG * P:(cG + 1) * P].rearrange("p (s j d) -> p j s d", j=J, s=SG))
                last.then_inc(v_w, 1)

            def layernorm(i, src, dst, done):
                nc.vector.tensor_scalar(dst, src, moments[:, i, 0:1], rstd[:, i:i + 1], ALU.subtract, ALU.mult).then_inc(done, 1)

            def maximum(k, par, g):
                dve.wait_ge(pe_S, 8 * k + g + 1)
                nc.vector.tensor_reduce(mx[par][:, J * g:J * g + J], S_ps[g % 2][:].rearrange("p (j t) -> p j t", j=J),
                                        AX_X, ALU.max).then_inc(v_max, 1)

            def normalise(k, G):
                src = (MA, MB)[G][:].rearrange("p (j s r) -> p j s r", j=J, s=SG)
                dve.wait_ge(pe_OT, 2 * k + G + 1)
                r = rec[:, G, :].rearrange("p (j s a) -> p j s a", j=J, a=1)
                nc.vector.reciprocal(r, src[:, :, :, HD:HD + 1]).then_inc(v_rec, 1)
                dve.wait_ge(v_rec, 2 * k + G + 1)
                wait(dve, pe_AT, k)
                nc.vector.tensor_tensor(attn[:, G * P:(G + 1) * P].rearrange("p (s j d) -> p j s d", s=SG, j=J),
                                        src[:, :, :, 0:HD], r.broadcast_to([P, J, SG, HD]), ALU.mult).then_inc(v_norm, 1)

            def hidden(v, half, i=0, n_cb=None):
                dve.wait_ge(pe_U, v + 1)
                dve.wait_ge(a_sil, v + 1)
                if n_cb is None:
                    wait(dve, v_hlo, v - 1)
                    nc.vector.tensor_tensor(hh[half][:], U_ps[:], sil[half][:], ALU.mult).then_inc(v_su, 1)
                    dve.wait_ge(v_su, v + 1)
                    nc.vector.engine_nop().then_inc(v_h, 1)
                else:
                    nc.vector.tensor_tensor(su[half][:], U_ps[:], sil[half][:], ALU.mult).then_inc(v_su, 1)
                    dve.wait_ge(v_su, v + 1)
                    dve.wait_ge(cb_in[i], n_cb)
                    nc.vector.tensor_tensor(hh[half][:], su[half][:], cb[i][:, half * HALF:(half + 1) * HALF],
                                            ALU.mult).then_inc(v_h, 1)
                dve.wait_ge(a_hhi, v + 1)
                nc.vector.tensor_tensor(hlo[half][:], hh[half][:], hhi[half][:].bitcast(F32), ALU.subtract).then_inc(v_hlo, 1)

            def body(n, odd, has):
                k1 = n + 1
                statistics(n, has)
                if has(n):
                    dve.wait_ge(pe_MT, n + 1)
                    wait(dve, pe_ST, 8 * n)
                    if isinstance(n, int) and n == 0:
                        dve.wait_ge(arrived["jmask"], 16)
                    nc.vector.tensor_tensor(Dm[:].rearrange("p (j t) -> p j t", j=J),
                                            S_ps[1][0:2 * HEADS, 0:T].rearrange("p (a t) -> p a t", a=1).broadcast_to([2 * HEADS, J, T]),
                                            jmask[:].rearrange("p (j a) -> p j a", a=1).broadcast_to([2 * HEADS, J, T]),
                                            ALU.mult).then_inc(v_D, 1)
                if has(k1):
                    dve.wait_ge(pe_QKT, 3 * k1 + 3)
                    wait(dve, pe_ST, 8 * k1 - 8)
                    nc.vector.tensor_copy(qT[1 - odd][:, J * T:], MB[:]).then_inc(v_qT, 1)
                for g in range(GROUPS):
                    if g in (1, 2) and has(n - 1):
                        normalise(n - 1, g - 1)
                    if g == 2 and n_is(n, FIRST_N):
                        query_weights()
                    if g == 0 and n_is(n, -1):
                        dve.wait_ge(arrived["onesel"], 16)
                        nc.vector.tensor_copy(onesel[:], onesel_raw[:]).then_inc(v_const, 1)
                    if g == 4 and n_is(n, 0):
                        dve.wait_ge(pe_w, 4)
                        nc.vector.tensor_copy(wrT[:], bank[5][:, 0:NC * E]).then_inc(v_w, 1)
                        dve.wait_ge(v_w, 2)
                        w = wrT[:].rearrange("p (c e) -> p c e", c=NC)
                        nc.vector.tensor_copy(wrT_hl[:, :, 0, :], w).then_inc(v_w, 1)
                        dve.wait_ge(v_w, 3)
                        nc.vector.tensor_tensor(wrT_hl[:, :, 1, :], w, wrT_hl[:, :, 0, :].bitcast(F32), ALU.subtract).then_inc(v_w, 1)
                        nc.vector.tensor_copy(w1T[:], bank[5][:, P:P + NC * P])
                        nc.vector.tensor_copy(w2T[:], bank[5][:, P + NC * P:P + NC * P + ND])
                        nc.vector.tensor_copy(affT[:], bank[5][0:ND, P + NC * P + 64:P + NC * P + 64 + E]).then_inc(v_w, 1)
                    if g == 1 and n_is(n, B + 1):
                        hidden(1, 1)
                    if g == 3 and n_is(n, B):
                        hidden(0, 0)
                    if g == 1:
                        dve.wait_ge(g_ln, LN_STEPS * (n - FIRST_N + 1))
                        if has(n + 2):
                            k = n + 2
                            wait(dve, pe_T1, k)
                            layernorm(0, x_all[:, bass.ds(k * D, D)], xn[:], v_xn)
                        if has(n - 2):
                            k = n - 2
                            wait(dve, pe_XT, k)
                            layernorm(1, xb_all[:, bass.ds(k * D, D)], x2n[:], v_x2n)
                    if g == 4 and has(n - 2):
                        k = n - 2
                        dve.wait_ge(a_x2hi, k + 1)
                        nc.vector.tensor_tensor(x2lo[:, :, bass.ds(k * T, T)], MA[:, 0:D].rearrange("p (c t) -> p c t", c=NC),
                                                x2hi[:, :, bass.ds(k * T, T)].bitcast(F32), ALU.subtract).then_inc(v_x2lo, 1)
                    if has(k1):
                        for i in SCORES_AT[g]:
                            maximum(k1, 1 - odd, i)
                    if g == 5 and has(n + 2):
                        k = n + 2
                        dve.wait_ge(a_qkv, k + 1)
                        kv = krep[:].rearrange("p (g r d) -> p g r d", g=GROUPS, r=4)
                        nc.vector.tensor_tensor(kv[:, :, 2:4, :],
                                                MA[:, D:D + 64].rearrange("p (g a d) -> p g a d", g=GROUPS, a=1)
                                                .broadcast_to([P, GROUPS, 2, HD]), kv[:, :, 0:2, :].bitcast(F32), ALU.subtract)
                        qv = qrep[:].rearrange("p (h r d) -> p h r d", h=HEADS, r=4)
                        nc.vector.tensor_tensor(qv[:, :, 1:4:2, :],
                                                MA[:, 0:D].rearrange("p (h a d) -> p h a d", h=HEADS, a=1)
                                                .broadcast_to([P, HEADS, 2, HD]), qv[:, :, 0:4:2, :].bitcast(F32),
                                                ALU.subtract).then_inc(v_lo, 1)
                if has(k1):
                    dve.wait_ge(v_max, 8 * k1 + 8)
                    m = mx[1 - odd][:].rearrange("p (h a) -> p h a", a=1)
                    wait(dve, pe_MT, k1)
                    nc.vector.tensor_scalar(ml[:, 0, :, 0:1], m, -1.0, None, ALU.mult).then_inc(v_mhi, 1)
                    dve.wait_ge(v_mhi, k1 + 1)
                    nc.vector.scalar_tensor_tensor(out=ml[:, 0, :, 1:2], in0=m, scalar=-1.0, in1=ml[:, 0, :, 0:1].bitcast(F32),
                                                   op0=ALU.mult, op1=ALU.subtract).then_inc(v_ml, 1)
                if has(n - 1):
                    k = n - 1
                    dve.wait_ge(pe_FC, k + 1)
                    if isinstance(k, int) and k == 0:
                        dve.wait_ge(g_xb, B)
                    row = xb_all[:, bass.ds(k * D, D)]
                    nc.vector.tensor_tensor(row, MB[:, 0:D], row, ALU.add).then_inc(v_x2, 1)
            iterations(dve, body)

            steps = []

            def step(name, ins):
                steps.append(name)
                ins.then_inc(v_gate, 1)
                dve.wait_ge(v_gate, gate_step(name))

            def logits_sum():
                for i in range(2):
                    b = slice(i * B // 2, (i + 1) * B // 2)
                    dve.wait_ge(a_lg, i + 1)
                    last = nc.vector.tensor_tensor(lg[:, b, :], ACC[1][i][:].rearrange("p (b m e) -> p b m e", b=B // 2, m=2)[:, :, 1, :],
                                                   lg_hi[:, b, :], ALU.add)
                step("logits without the domains' share", last)

            def domains_in():
                dve.wait_ge(pe_td, 1)
                dve.wait_ge(arrived["b2"], 16)
                step("domain logits", nc.vector.tensor_tensor(td[:], MB[0:B, 0:ND], b2_b[:], ALU.add))
                step("their maximum", nc.vector.tensor_reduce(tdm[:], td[:], AX_X, ALU.max))
                step("domain logits less their maximum", nc.vector.tensor_scalar(td[:], td[:], tdm[:, 0:1], None, ALU.subtract))

            def domains_out():
                dve.wait_ge(a_td, 1)
                step("one over the domains' sum", nc.vector.reciprocal(tdr[:], tds[:]))
                step("half the domain shares", nc.vector.tensor_scalar(tdn[:], td[:], tdr[:, 0:1], 0.5, ALU.mult, ALU.mult))

            def domains_spread():
                dve.wait_ge(pe_tdT, 1)
                step("shares by domain", nc.vector.tensor_copy(tdT[:], MA[0:ND, 0:B]))
                step("shares for every token", nc.vector.tensor_copy(
                    tdb[:].rearrange("p (b t) -> p b t", b=B), tdT[:].rearrange("p (b a) -> p b a", a=1).broadcast_to([ND, B, T])))

            def logits_whole():
                dve.wait_ge(pe_dom, 1)
                dve.wait_ge(arrived["rbias"], 16)
                step("logits", nc.vector.tensor_tensor(lg[:], MB[:].rearrange("p (b e) -> p b e", b=B), lg[:], ALU.add))
                step("largest logit", nc.vector.tensor_reduce(lmax[:], lg[:], AX_X, ALU.max))
                step("its negative", nc.vector.tensor_scalar(minus_lmax[:], lmax[:], -1.0, None, ALU.mult))

            def largest_biased():
                dve.wait_ge(g_const, 5)
                step("logits with bias", nc.vector.tensor_tensor(
                    lb[:, :, 0:E], lg[:], rbias_b[:].rearrange("p (a e) -> p a e", a=1).broadcast_to([P, B, E]), ALU.add))
                for b in range(B):
                    ins = nc.vector.max(top[:, b, :], lb[:, b, 0:E])
                step("eight largest", ins)
                step("four largest and fillers", nc.vector.memset(top[:, :, TOPK:8], FAR))

            def chosen():
                for b in range(B):
                    ins = nc.vector.match_replace(rep[:, b, :], top[:, b, :], lb[:, b, :], -FAR)
                step("four largest struck out", ins)
                step("chosen", nc.vector.tensor_tensor(sel[:], rep[:, :, 0:E], lb[:, :, 0:E], ALU.not_equal))

            def combine():
                dve.wait_ge(a_ex, 1)
                step("exp of the chosen", nc.vector.tensor_tensor(ex[:], ex[:], sel[:], ALU.mult))
                step("their sum", nc.vector.tensor_reduce(z_top[:], ex[:], AX_X, ALU.add))
                step("guarded sum", nc.vector.scalar_tensor_tensor(out=z_all[:], in0=z_all[:], scalar=GUARD, in1=z_top[:],
                                                                   op0=ALU.mult, op1=ALU.add))
                step("one over it", nc.vector.reciprocal(z_top[:], z_all[:]))
                step("combine weights", nc.vector.tensor_tensor(
                    cw[:], ex[:], z_top[:].rearrange("p (b a) -> p b a", a=1).broadcast_to([P, B, E]), ALU.mult))

            def combine_by_expert():
                for i, m in enumerate((MA, MB)):
                    dve.wait_ge(pe_cT, i + 1)
                    last = nc.vector.tensor_copy(cT[:, i * HALF:(i + 1) * HALF], m[0:E, :])
                step("combine weights by expert", last)

            hidden(2, 0)
            logits_sum()
            domains_in()
            domains_out()
            hidden(3, 1)
            domains_spread()
            logits_whole()
            hidden(4, 0)
            largest_biased()
            hidden(5, 1)
            chosen()
            hidden(6, 0)
            combine()
            combine_by_expert()
            hidden(7, 1)
            assert tuple(steps) == GATE, steps
            with dve.Fori((SHARED_UNITS) // 2, (UNITS) // 2) as t:
                u = 2 * t
                for i in range(2):
                    for half in range(2):
                        hidden(2 * (u + i) + half, half, i, 16 * (u - SHARED_UNITS) + 32)
            dve.wait_ge(pe_D, 2 * UNITS)
            for half in range(2):
                nc.vector.tensor_copy(yT[:, 1, half * HALF:(half + 1) * HALF], ACC[half][1][:]).then_inc(v_yT, 1)
            for q in range(4):
                dve.wait_ge(pe_Y, q + 1)
                nc.vector.tensor_tensor(y[:, 2 * q * D:(2 * q + 2) * D], bank[q % 2][:],
                                        xb_all[:, 2 * q * D:(2 * q + 2) * D], ALU.add).then_inc(v_y, 1)

        @block.tensor
        def _(pe):
            mm = nc.tensor.matmul

            def turn(out_, in_):
                k = in_.shape[0]
                return nc.tensor.transpose(out_, in_, ident[0:k, 0:k])

            pe.wait_ge(arrived["ident"], 16)
            pe.wait_ge(arrived["wq"], 16)
            for c in range(NC):
                for a in range(NC):
                    last = turn(bank[0][:, (c * NC + a) * P:(c * NC + a + 1) * P], wq_n[:, a, c * P:(c + 1) * P])
            last.then_inc(pe_w, 1)
            pe.wait_ge(arrived["wkv"], 32)
            for c in range(NC):
                last = turn(bank[1][:, c * P:(c + 1) * P], wkv_n[:, c * P:(c + 1) * P])
            last.then_inc(pe_w, 1)

            def later_weights():
                pe.wait_ge(arrived["wfc"], 16)
                for c in range(NC):
                    for a in range(NC):
                        last = turn(bank[4][:, (c * NC + a) * P:(c * NC + a + 1) * P], wfc_n[:, a, c * P:(c + 1) * P])
                last.then_inc(pe_w, 1)
                for n_ in ("wr", "w1", "w2", "aff"):
                    pe.wait_ge(arrived[n_], 16)
                for c in range(NC):
                    turn(bank[5][:, c * E:(c + 1) * E], wr_n[:, c:D:NC])
                for c in range(NC):
                    turn(bank[5][:, P + c * P:P + (c + 1) * P], w1_n[:, c:D:NC])
                turn(bank[5][:, P + NC * P:P + NC * P + ND], w2_n[:])
                turn(bank[5][0:ND, P + NC * P + 64:P + NC * P + 64 + E], aff_n[:]).then_inc(pe_w, 1)

            def rows(s):
                return slice(s * STRIP, (s + 1) * STRIP)

            def product(out_, w_hi, w_lo, r_hi, r_lo, chunks, first, last_):
                n_ = 3 * len(chunks)
                i = 0
                for c in chunks:
                    for w, r in ((w_hi, r_hi), (w_hi, r_lo), (w_lo, r_hi)):
                        ins = mm(out_, w(c), r(c), start=(first and i == 0), stop=(last_ and i == n_ - 1))
                        i += 1
                return ins

            def gate_or_up(v, half, i, m):
                t = slice(half * HALF, (half + 1) * HALF)
                bank_, free, done = ((G_ps, a_sil, pe_G), (U_ps, v_su, pe_U))[m]
                wait(pe, free, v)
                product(bank_[:], lambda c: whi[i][:, m * D + c * P:m * D + (c + 1) * P],
                        lambda c: wlo[i][:, m * D + c * P:m * D + (c + 1) * P],
                        lambda c: x2hi[:, c, t], lambda c: x2lo[:, c, t], range(NC), True, True).then_inc(done, 1)

            def down(v, half, i, h, first=False, last_=False):
                pe.wait_ge(v_hlo, v + 1)
                for dh in range(NC):
                    ins = product(ACC[half][dh][:], lambda c: whi[i][:, 2 * D + dh * P:2 * D + (dh + 1) * P],
                                  lambda c: wlo[i][:, 2 * D + dh * P:2 * D + (dh + 1) * P],
                                  lambda c: hhi[h][:], lambda c: hlo[h][:], range(1), first, last_)
                ins.then_inc(pe_D, 1)

            def shared_gate(v):
                half, u = divmod(v, SHARED_UNITS)
                if half == 0:
                    pe.wait_ge(g_wlo, u + 1)
                gate_or_up(v, half, u, 0)

            def shared_up(v):
                half, u = divmod(v, SHARED_UNITS)
                gate_or_up(v, half, u, 1)

            def shared_down(v):
                half, u = divmod(v, SHARED_UNITS)
                if v == SHARED_UNITS:
                    pe.wait_ge(v_gate, gate_step("logits without the domains' share"))
                down(v, half, u, v % 2, first=(u == 0))

            def body(n, odd, has):
                def scores_by_query(i):
                    k, G, o = n + 1, i // J, 1 - odd
                    if i == 0:
                        pe.wait_ge(a_kT, k + 1)
                        pe.wait_ge(a_qT, k + 1)
                    if i == 1:
                        wait(pe, v_D, k)
                    if i == J:
                        pe.wait_ge(v_qT, k + 1)
                    if i > 1:
                        pe.wait_ge(v_max, 8 * k + i - 1)
                    mm(S_ps[i % 2][:], qT[o][:, i * T:(i + 1) * T], kT[o][:, G * SG * T:(G + 1) * SG * T],
                       start=True, stop=True).then_inc(pe_S, 1)

                def scores_by_key(g):
                    G = g // SG
                    if g == 0:
                        pe.wait_ge(v_D, n + 1)
                        if isinstance(n, int) and n == 0:
                            pe.wait_ge(v_const, 2)
                    wait(pe, a_exp, 8 * n + g - 1)
                    mm(ST_ps[g % 2][:], kT[odd][:, g * T:(g + 1) * T], qT[odd][:, G * J * T:(G + 1) * J * T],
                       start=True, stop=False)
                    mm(ST_ps[g % 2][:], onesel[:, g * P:(g + 1) * P], Dm[:], start=False, stop=True).then_inc(pe_ST, 1)

                def values(k, par, G):
                    pe.wait_ge(a_V, k + 1)
                    pe.wait_ge(a_exp, 8 * k + SG * G + SG)
                    wait(pe, a_O, 2 * k - 1 + G)
                    if n_is(k, 0):
                        pe.wait_ge(*((a_w, 2), (v_w, 5))[G])
                    for s in range(SG):
                        g = SG * G + s
                        last = mm(O_ps[G][rows(s), :], Vw[par][:, g * STRIP:(g + 1) * STRIP], Pr[g], start=True, stop=True)
                    last.then_inc(pe_PV, 1)

                def heads_by_query(k, G):
                    pe.wait_ge(a_O, 2 * k + G + 1)
                    for j in range(J):
                        last = turn((MA, MB)[G][:, j * P:(j + 1) * P], O_sb[G][:, j * T:(j + 1) * T])
                    last.then_inc(pe_OT, 1)

                def query_operand(k, G):
                    for j in range(J):
                        last = turn((MA, MB)[G][:, j * T:(j + 1) * T],
                                    qrep[:, (G * J + j) * P:(G * J + j + 1) * P].bitcast(F32))
                    last.then_inc(pe_QKT, 1)

                if has(n + 1):
                    k = n + 1
                    pe.wait_ge(v_lo, k + 1)
                    wait(pe, v_max, 8 * k - 1)
                    for G in range(NG):
                        last = turn(S_ps[0][:, G * T:(G + 1) * T], krep[:, G * P:(G + 1) * P].bitcast(F32))
                    last.then_inc(pe_QKT, 1)
                    query_operand(k, 0)
                if has(n):
                    pe.wait_ge(v_ml, n + 1)
                    if isinstance(n, int) and n == 0:
                        pe.wait_ge(g_const, 3)
                    turn(S_ps[1][:, 0:T], ml[:].rearrange("p z h a -> p (z h a)").bitcast(F32)).then_inc(pe_MT, 1)
                if has(n - 1):
                    values(n - 1, 1 - odd, 1)
                if has(n + 1):
                    wait(pe, v_x2, n - 1)
                    query_operand(n + 1, 1)
                for g in range(GROUPS):
                    if g == 2 and n_is(n, -1):
                        later_weights()
                    if has(n):
                        scores_by_key(g)
                    if g == 1 and has(n - 1):
                        if has(n + 1):
                            pe.wait_ge(a_qT, n + 2)
                        else:
                            pe.wait_ge(v_x2lo, n - 2)
                        heads_by_query(n - 1, 0)
                    if g == 2 and has(n - 1):
                        if has(n + 1):
                            pe.wait_ge(v_qT, n + 2)
                        else:
                            pe.wait_ge(v_x2, n - 1)
                        heads_by_query(n - 1, 1)
                    if g == 4 and n_is(n, B + 1):
                        shared_gate(2)
                    if g == 3 and has(n + 2):
                        k = n + 2
                        pe.wait_ge(ctx_arrived[odd], 8 * (k - odd) + 16)
                        if has(n - 1):
                            pe.wait_ge(v_norm, 2 * n)
                        elif has(n + 1):
                            pe.wait_ge(v_qT, n + 2)
                        pe.wait_ge(v_xn, k + 1)
                        for c in range(NC):
                            turn(MB[:, c * T:(c + 1) * T], xn[:, c * P:(c + 1) * P])
                        for c in range(NC):
                            last = turn(MB[:, D + c * T:D + (c + 1) * T], ctx_in[odd][:, c * P:(c + 1) * P])
                        last.then_inc(pe_T1, 1)
                    if g == 4 and has(n - 2):
                        k = n - 2
                        pe.wait_ge(v_x2n, k + 1)
                        if isinstance(k, int) and k == 0:
                            pe.wait_ge(g_const, 4)
                        if has(n - 1):
                            pe.wait_ge(v_norm, 2 * (n - 1) + 1)
                        else:
                            pe.wait_ge(v_x2lo, n - 2)
                        for c in range(NC):
                            turn(MA[:, c * T:(c + 1) * T], x2n[:, c:D:NC])
                        for c in range(NC):
                            last = mm(MA[:, D + c:D + c + 1], x2n[:, c:D:NC], inv_t[:, 0:1], start=True, stop=True)
                        last.then_inc(pe_XT, 1)
                    if g == 4 and n_is(n, B):
                        shared_gate(1)
                    if g == 4 and n_is(n, B + 1):
                        shared_up(2)
                    if g == 4 and has(n - 1):
                        pe.wait_ge(v_norm, 2 * n)
                        if has(n + 2):
                            pe.wait_ge(a_xcT, n + 3)
                        for c in range(NC):
                            last = turn(MB[:, c * T:(c + 1) * T], attn[:, c * P:(c + 1) * P])
                        last.then_inc(pe_AT, 1)
                    if g == 5 and has(n + 2):
                        k = n + 2
                        pe.wait_ge(a_xcT, k + 1)
                        if n_is(k, 0):
                            pe.wait_ge(v_w, 1)
                            pe.wait_ge(a_w, 1)
                        if has(n - 2):
                            pe.wait_ge(v_x2lo, n - 1)
                        elif has(n - 1):
                            pe.wait_ge(v_norm, 2 * (n - 1) + 1)
                        elif has(n + 1):
                            pe.wait_ge(a_qT, n + 2)
                        for c in range(NC):
                            mm(MA[:, 0:D], xcT[:, c * T:(c + 1) * T], wqT[:, c * D:(c + 1) * D], start=(c == 0), stop=(c == NC - 1))
                        for c in range(NC):
                            last = mm(MA[:, D:D + P], xcT[:, D + c * T:D + (c + 1) * T], wkvT[:, c * P:(c + 1) * P],
                                      start=(c == 0), stop=(c == NC - 1))
                        last.then_inc(pe_PJ, 1)
                    if g == 5 and has(n):
                        values(n, odd, 0)
                    if g == 7 and n_is(n, B):
                        shared_up(1)
                    if g == 7 and has(n - 1):
                        pe.wait_ge(a_attnT, n)
                        for c in range(NC):
                            last = mm(MB[:, 0:D], attnT[:, c * T:(c + 1) * T], wfcT[:, c * D:(c + 1) * D],
                                      start=(c == 0), stop=(c == NC - 1))
                        last.then_inc(pe_FC, 1)
                    if has(n + 1):
                        for i in SCORES_AT[g]:
                            scores_by_query(i)
                if n_is(n, B - 1):
                    shared_gate(0)
                    shared_up(0)
                if n_is(n, B):
                    shared_down(0)

            iterations(pe, body)

            def logits():
                pe.wait_ge(v_x2lo, B)
                for b in range(B):
                    o = ACC[1][b // (B // 2)][:, (b % (B // 2)) * 2 * E:(b % (B // 2) + 1) * 2 * E]
                    parts = [(c, xs) for c in range(NC) for xs in (x2hi, x2lo)]
                    for i, (c, xs) in enumerate(parts):
                        last = mm(o, xs[:, c, b * T:(b + 1) * T], wrT_hl[:, c].rearrange("p m e -> p (m e)"),
                                  start=(i == 0), stop=(i == len(parts) - 1))
                    if b % (B // 2) == B // 2 - 1:
                        last.then_inc(pe_lg, 1)

            def domains_hidden():
                for c in range(NC):
                    last = mm(MA[:, 0:B], w1T[:, c * P:(c + 1) * P], xmT[:, c, :], start=(c == 0), stop=(c == NC - 1))
                last.then_inc(pe_h1, 1)

            def domains_logits():
                pe.wait_ge(a_h1, 1)
                mm(MB[0:B, 0:ND], h1T[:], w2T[:], start=True, stop=True).then_inc(pe_td, 1)

            def domains_turn():
                pe.wait_ge(v_gate, gate_step("half the domain shares"))
                turn(MA[0:ND, 0:B], tdn[:]).then_inc(pe_tdT, 1)

            def domains_share():
                pe.wait_ge(v_gate, gate_step("shares for every token"))
                for b in range(B):
                    last = mm(MB[:, b * E:(b + 1) * E], tdb[:, b * T:(b + 1) * T], affT[:], start=True, stop=True)
                last.then_inc(pe_dom, 1)

            def combine_turn():
                pe.wait_ge(v_gate, gate_step("combine weights"))
                for b in range(B):
                    m = (MA, MB)[b // (B // 2)]
                    last = turn(m[0:E, (b % (B // 2)) * T:(b % (B // 2) + 1) * T], cw[:, b, :])
                    if b % (B // 2) == B // 2 - 1:
                        last.then_inc(pe_cT, 1)

            logits()
            domains_hidden()
            shared_down(1)
            gate = {(3, 0): domains_logits, (3, 2): domains_turn, (4, 0): domains_share, (7, 0): combine_turn}
            for v in range(EARLY, SHARED_STEPS):
                for part, piece in enumerate((shared_gate, shared_up, lambda v: shared_down(v - 1))):
                    piece(v)
                    if (v, part) in gate:
                        gate[v, part]()

            def two_units(u, first=False, final=False):
                for i in range(2):
                    pe.wait_ge(g_wlo, u + i + 1)
                    for half in range(2):
                        v = 2 * (u + i) + half
                        gate_or_up(v, half, i, 0)
                        gate_or_up(v, half, i, 1)
                        if first and i + half == 0:
                            shared_down(v - 1)
                        else:
                            down(v - 1, 1 - half, i if half else 1 - i, 1 - half, last_=(final and i == 1 and half == 1))

            two_units(SHARED_UNITS, first=True)
            with pe.Fori((SHARED_UNITS + 2) // 2, UNITS // 2 - 1) as t:
                two_units(2 * t)
            two_units(UNITS - 2, final=True)
            down(2 * UNITS - 1, 1, 1, 1, last_=True)
            pe.wait_ge(a_yT, 2)
            pe.wait_ge(v_yT, 2)
            for q in range(4):
                if q >= 2:
                    pe.wait_ge(v_y, q - 1)
                for b in (2 * q, 2 * q + 1):
                    for dh in range(NC):
                        last = turn(bank[q % 2][:, (b % 2) * D + dh * P:(b % 2) * D + (dh + 1) * P],
                                    yT[:, dh, b * T:(b + 1) * T])
                last.then_inc(pe_Y, 1)


_INS = ["x", "ctx_2048", "L0_xattn_Wq", "L0_xattn_Wk", "L0_xattn_Wv", "L0_xattn_Wfc", "L0_xattn_bfc", "L0_ffn_Wr",
        "L0_ffn_router_bias", "L0_ffn_affinity", "L0_ffn_te_W1", "L0_ffn_te_b1", "L0_ffn_te_W2", "L0_ffn_te_b2",
        "L0_ffn_Wg", "L0_ffn_Wu", "L0_ffn_Wd", "L0_ffn_Sg", "L0_ffn_Su", "L0_ffn_Sd"]


def kernel(**inputs):
    import numpy as _np
    import concourse.bacc as _bacc
    from concourse import mybir as _mybir
    from concourse.bass_utils import run_bass_kernel_spmd as _run

    nc = _bacc.Bacc("TRN2", target_bir_lowering=False, num_devices=1)
    arrays = {f"in_{n}": _np.ascontiguousarray(inputs[n]) for n in _INS}
    rows = _np.arange(2 * HEADS)
    group = rows // (2 * SG * J) * SG + rows // 2 % SG
    arrays["const_ident"] = _np.eye(P, dtype=_np.float32)
    arrays["const_onesel"] = _np.repeat((group[:, None] == _np.arange(GROUPS)[None]).astype(_np.float32), P, axis=1)
    arrays["const_jmask"] = (rows[:, None] // (2 * SG) % J == _np.arange(J)[None]).astype(_np.float32)
    args = [nc.dram_tensor(n, a.shape, _mybir.dt.from_np(a.dtype), kind="ExternalInput").ap() for n, a in arrays.items()]
    out = nc.dram_tensor("out_0", (B, T, D), _mybir.dt.float32, kind="ExternalOutput").ap()
    build(nc, *args, out)
    result = _run(nc, [arrays], core_ids=[0])
    return result.results[0]["out_0"]
```

```python
from contextlib import ExitStack

import concourse.bass as bass
from concourse import mybir

F32 = mybir.dt.float32
F32R = mybir.dt.float32r
I32 = mybir.dt.int32
ACT = mybir.ActivationFunctionType
ALU = mybir.AluOpType
AX_X = mybir.AxisListType.X

P = 128
B, T, D = 8, 128, 256
NC = D // P
HEADS, GROUPS = 32, 8
J = HEADS // GROUPS
HD = D // HEADS
STRIP = 32
SG = P // STRIP
NG = GROUPS // SG
E, F = 64, 64
TOPK = 4
H_SHARED = 256
N_SHARED = 2
ND = 4
TOK = B * T
HALF = TOK // 2
SHARED_UNITS = N_SHARED * H_SHARED // P
EXPERT_UNITS = E * F // P
UNITS = SHARED_UNITS + EXPERT_UNITS
SHARED_STEPS = 2 * SHARED_UNITS
EARLY = 3
EPS = 1e-5
SCALE = float(HD) ** -0.5
GUARD = 1e-8
FAR = 3.0e38


TOP = ("logits with bias", "eight largest", "four largest and fillers")
STRIKE = ("four largest struck out", "chosen")
COMBINE = ("sum of exp", "exp of the chosen", "their sum", "guarded sum", "one over it", "combine weights")
BY_EXPERT = ("combine weights by expert",)
GATE = ("domain logits", "their maximum", "domain logits less their maximum", "one over the domains' sum",
        "half the domain shares", "logits without the domains' share", "shares by domain", "shares for every token",
        "logits", "largest logit") + tuple(
            (name, h) for h, names in ((0, TOP), (0, STRIKE), (1, TOP), (0, COMBINE), (0, BY_EXPERT), (1, STRIKE),
                                       (1, COMBINE), (1, BY_EXPERT)) for name in names)
LN_STEPS = 7


def gate_step(name):
    return GATE.index(name) + 1


def build(nc, x, ctx, Wq, Wk, Wv, Wfc, bfc, Wr, rbias, aff, W1, b1, W2, b2, Wg, Wu, Wd, Sg, Su, Sd,
          ident_d, out):
    c_dram = nc.dram_tensor("combine_scratch", (E, TOK), F32, kind="Internal").ap()
    with ExitStack() as stack:
        def sb(name, shape, dt=F32):
            return stack.enter_context(nc.sbuf_tensor(name, shape, dt))

        def sem(name):
            return stack.enter_context(nc.semaphore(name))

        bank = [stack.enter_context(nc.psum_tensor(f"bank{i}", [P, 512], F32)) for i in range(8)]
        S_ps, ST_ps = bank[0:2], bank[2:4]
        O_ps, MA, MB = bank[4:6], bank[6], bank[7]
        G_ps, U_ps = bank[0], bank[1]
        Y_ps = [MA, MB, bank[0], bank[1]]
        ACC = [bank[2:4], bank[4:6]]

        ident = sb("ident", [P, P])
        ident_r = sb("ident_r", [P, P], F32R)
        inv_t = sb("inv_t", [P, 2])
        zeros = sb("zeros", [P, HEADS, 2])
        wq_n = sb("wq_n", [P, NC, D])
        wfc_n = sb("wfc_n", [P, NC, D])
        wkv_n = sb("wkv_n", [P, D])
        wr_n = sb("wr_n", [E, D])
        w1_n = sb("w1_n", [P, D])
        w2_n = sb("w2_n", [ND, P])
        aff_n = sb("aff_n", [E, ND])
        wqT = sb("wqT", [P, NC * D])
        wfcT = sb("wfcT", [P, NC * D])
        wkvT = sb("wkvT", [P, NC * P])
        wrT = sb("wrT", [P, NC * E])
        wrT_hl = sb("wrT_hl", [P, NC, 2, E], F32R)
        w1T = sb("w1T", [P, NC * P])
        w2T = sb("w2T", [P, ND])
        affT = sb("affT", [ND, E])
        bfc_b = sb("bfc_b", [P, D])
        b1_c = sb("b1_c", [P, 1])
        b2_b = sb("b2_b", [B, ND])
        rbias_b = sb("rbias_b", [P, E])

        x_all = sb("x_all", [P, B * D])
        ctx_in = [sb(f"ctx_in{i}", [P, D]) for i in range(2)]
        xb_all = sb("xb_all", [P, B * D])
        LN2 = B
        stats = sb("stats", [P, B + 1, 2, 3])
        terms = sb("terms", [P, B + 1, 3])
        moments = sb("moments", [P, B + 1, 3])
        moment_of = sb("moment_of", [P, B + 1, 3])
        apart = sb("apart", [P, B + 1])
        var = sb("var", [P, B + 1])
        eps = sb("eps", [P, B + 1])
        minus_half = sb("minus_half", [P, B + 1])
        rstd = sb("rstd", [P, B + 1])
        xn = sb("xn", [P, D])
        xcT = sb("xcT", [P, 2 * D])
        qrep = [sb(f"qrep{i}", [P, HEADS * STRIP], F32R) for i in range(2)]
        krep = sb("krep", [P, GROUPS * STRIP], F32R)
        qT = [sb(f"qT{i}", [P, NG * J * T], F32R) for i in range(2)]
        kT = [sb(f"kT{i}", [P, NG * SG * T], F32R) for i in range(2)]
        HALF_STRIP = STRIP // NG
        Vw = [sb(f"Vw{i}", [P, NG, HALF_STRIP + SG * STRIP]) for i in range(2)]
        v_sb = sb("v_sb", [P, GROUPS * HD])
        mx = [sb(f"mx{i}", [P, HEADS]) for i in range(2)]
        Pr_all = sb("Pr_all", [P, GROUPS * J * T])
        Pr = [Pr_all[:, g * J * T:(g + 1) * J * T] for g in range(GROUPS)]
        O_sb = sb("O_sb", [P, J * T])
        rec = sb("rec", [P, HEADS])
        attn = sb("attn", [P, D])
        attnT = sb("attnT", [P, D])
        x2n = sb("x2n", [P, D])
        x2hi = sb("x2hi", [P, NC, TOK], F32R)
        x2lo = sb("x2lo", [P, NC, TOK], F32R)
        xmT = sb("xmT", [P, NC, B])

        h1T = sb("h1T", [P, B])
        td = sb("td", [B, ND])
        tdm = sb("tdm", [B, 1])
        tds = sb("tds", [B, 1])
        tdr = sb("tdr", [B, 1])
        tdn = sb("tdn", [B, ND])
        tdT = sb("tdT", [ND, B])
        tdb = sb("tdb", [ND, B * T])
        lg_hi = sb("lg_hi", [P, B, E])
        lg = sb("lg", [P, B, E])
        lb = sb("lb", [P, B, E + 8])
        top = sb("top", [P, B, 8])
        rep = sb("rep", [P, B, E + 8])
        sel = sb("sel", [P, B, E])
        lmax = sb("lmax", [P, B])
        ex = sb("ex", [P, B, E])
        z_all = sb("z_all", [P, B])
        z_top = sb("z_top", [P, B])
        cw = sb("cw", [P, B, E])
        cT = sb("cT", [E, TOK])

        raw = [sb(f"raw{i}", [P, 3 * D]) for i in range(2)]
        whi = [sb(f"whi{i}", [P, 3 * D], F32R) for i in range(SHARED_UNITS)]
        wlo = [sb(f"wlo{i}", [P, 3 * D], F32R) for i in range(SHARED_UNITS)]
        cb = [sb(f"cb{i}", [P, TOK]) for i in range(2)]
        sil = [sb(f"sil{i}", [P, HALF]) for i in range(2)]
        su = [sb(f"su{i}", [P, HALF]) for i in range(2)]
        hh = [sb(f"hh{i}", [P, HALF]) for i in range(2)]
        hhi = [sb(f"hhi{i}", [P, HALF], F32R) for i in range(2)]
        hlo = [sb(f"hlo{i}", [P, HALF], F32R) for i in range(2)]
        yT = Pr_all[:, 0:NC * TOK].rearrange("p (c t) -> p c t", c=NC)
        y = x_all

        NW = ["ident", "wq", "wkv", "wfc", "wr", "w1", "w2", "aff", "bfc", "b1", "b2", "rbias"]
        arrived = {n: sem(f"arrived_{n}") for n in NW}
        x_first, x_rest = sem("x_first"), sem("x_rest")
        ctx_arrived = [sem(f"ctx_arrived{i}") for i in range(2)]
        raw_in = [sem(f"raw_in{i}") for i in range(2)]
        cb_in = [sem(f"cb_in{i}") for i in range(2)]
        cb_first = sem("cb_first")
        c_out = [sem(f"c_out{h}") for h in range(2)]
        y_out = sem("y_out")
        pe_w = sem("pe_w")
        pe_T1, pe_PJ, pe_QKT, pe_S, pe_qm0, pe_qm1, pe_ST, pe_PV, pe_OT, pe_AT, pe_FC, pe_XT = (
            sem(f"pe_{n}") for n in ("T1", "PJ", "QKT", "S", "qm0", "qm1", "ST", "PV", "OT", "AT", "FC", "XT"))
        pe_lg, pe_h1, pe_td, pe_tdT, pe_dom, pe_cT = (sem(f"pe_{n}") for n in ("lg", "h1", "td", "tdT", "dom", "cT"))
        pe_G, pe_U, pe_D, pe_Y = (sem(f"pe_{n}") for n in ("G", "U", "D", "Y"))
        a_w, a_xcT, a_qkv, a_V, a_kT, a_qT, a_qm, a_exp, a_O, a_attnT, a_x2hi = (
            sem(f"a_{n}") for n in ("w", "xcT", "qkv", "V", "kT", "qT", "qm", "exp", "O", "attnT", "x2hi"))
        a_lg, a_h1, a_td, a_ex, a_sil, a_hhi, a_whi, a_yT = (sem(f"a_{n}") for n in ("lg", "h1", "td", "ex", "sil", "hhi", "whi", "yT"))
        (v_w, v_stats, v_xn, v_lo, v_qT, v_max, v_mhi, v_ml, v_qm, v_rec, v_norm, v_x2, v_x2n, v_x2lo, v_ident, v_zero) = (
            sem(f"v_{n}") for n in ("w", "stats", "xn", "lo", "qT", "max", "mhi", "ml", "qm", "rec", "norm",
                                    "x2", "x2n", "x2lo", "ident", "zero"))
        v_gate, v_su, v_h, v_hlo, v_yT, v_y = (sem(f"v_{n}") for n in ("gate", "su", "h", "hlo", "yT", "y"))
        g_const, g_xb, g_ln, g_gate, g_clear, g_wlo = (sem(f"g_{n}") for n in ("const", "xb", "ln", "gate", "clear", "wlo"))

        FIRST_N, LAST_N = -2, B + 1
        LOOP = (2, 6)

        def iterations(eng, body):
            def has(k):
                return 0 <= k < B
            for n in range(FIRST_N, LOOP[0]):
                body(n, n % 2, has)
            with eng.Fori(LOOP[0] // 2, LOOP[1] // 2) as t:
                n = 2 * t
                body(n, 0, lambda k: True)
                body(n + 1, 1, lambda k: True)
            for n in range(LOOP[1], LAST_N + 1):
                body(n, n % 2, has)

        SPLIT_AT = {-1: (0, 1), 0: (2,), 1: (3,)}

        SCORES_AT = ((0,), (1,), (2,), (3,), (4,), (5, 6), (7,), ())

        def minus_maxima(i, lo, hi):
            return qrep[i][:].rearrange("p (h r d) -> p h r d", h=HEADS, r=4)[:, :, 3, lo:hi]

        def n_is(n, value):
            return isinstance(n, int) and n == value

        def wait(eng, s, value):
            if isinstance(value, int) and value <= 0:
                return
            eng.wait_ge(s, value)

        block = stack.enter_context(nc.Block())

        @block.sync
        def _(sp):
            sp.dma_start(x_all[:, 0:D], x[0]).then_inc(x_first, 16)
            sp.dma_start(ident[:], ident_d).then_inc(arrived["ident"], 16)
            sp.dma_start(wq_n[:], Wq.rearrange("(a p) i -> p a i", p=P)).then_inc(arrived["wq"], 16)
            sp.dma_start(ctx_in[0][:], ctx[0]).then_inc(ctx_arrived[0], 16)
            sp.dma_start(wkv_n[0:64, :], Wk).then_inc(arrived["wkv"], 16)
            sp.dma_start(wkv_n[64:128, :], Wv).then_inc(arrived["wkv"], 16)
            sp.dma_start(x_all[:, D:].rearrange("p (b d) -> p b d", b=B - 1),
                         x[1:B].rearrange("b p d -> p b d")).then_inc(x_rest, 16)
            sp.dma_start(ctx_in[1][:], ctx[1]).then_inc(ctx_arrived[1], 16)
            sp.dma_start(wfc_n[:], Wfc.rearrange("(a p) i -> p a i", p=P)).then_inc(arrived["wfc"], 16)
            sp.dma_start(wr_n[:], Wr).then_inc(arrived["wr"], 16)
            sp.dma_start(w1_n[:], W1).then_inc(arrived["w1"], 16)
            sp.dma_start(w2_n[:], W2).then_inc(arrived["w2"], 16)
            sp.dma_start(aff_n[:], aff).then_inc(arrived["aff"], 16)
            sp.dma_start(bfc_b[:], bfc.rearrange("(a n) -> a n", a=1).broadcast_to([P, D])).then_inc(arrived["bfc"], 16)
            sp.dma_start(b1_c[:], b1.rearrange("(p a) -> p a", a=1)).then_inc(arrived["b1"], 16)
            sp.dma_start(b2_b[:], b2.rearrange("(a n) -> a n", a=1).broadcast_to([B, ND])).then_inc(arrived["b2"], 16)
            sp.dma_start(rbias_b[:], rbias.rearrange("(a n) -> a n", a=1).broadcast_to([P, E])).then_inc(arrived["rbias"], 16)

            def load_unit(i, gate_up, down):
                for m in range(2):
                    dst = raw[i][:, m * D:(m + 1) * D]
                    src = gate_up[m]
                    if len(src.shape) == 4:
                        sp.dma_start(dst.rearrange("p (e c f) -> p e c f", e=2, c=NC), src).then_inc(raw_in[i], 16)
                    else:
                        sp.dma_start(dst.rearrange("p (c f) -> p c f", c=NC), src).then_inc(raw_in[i], 16)
                sp.dma_start(raw[i][:, 2 * D:3 * D], down).then_inc(raw_in[i], 16)

            def shared(u):
                s, h = divmod(u, H_SHARED // P)
                cols = slice(h * P, (h + 1) * P)
                return ([w[s, :, cols].rearrange("(p c) f -> p c f", c=NC) for w in (Sg, Su)],
                        Sd[s, h * P:(h + 1) * P, :])

            def experts(u):
                e = 2 * (u - SHARED_UNITS)
                return ([w[bass.ds(e, 2)].rearrange("e (p c) f -> p e c f", c=NC) for w in (Wg, Wu)],
                        Wd.rearrange("e f d -> (e f) d")[bass.ds(e * F, P), :])

            def load_combine(i, u):
                e = 2 * (u - SHARED_UNITS)
                for k in range(2):
                    sp.dma_start(cb[i][k * F:(k + 1) * F, :],
                                 c_dram[bass.ds(e + k, 1), :].broadcast_to([F, TOK])).then_inc(cb_in[i], 16)

            for u in range(2):
                load_unit(u, *shared(u))

            def load_ctx(t):
                for i in range(2):
                    sp.wait_ge(pe_T1, 2 * t + i - 1)
                    sp.dma_start(ctx_in[i][:], ctx.rearrange("b p d -> (b p) d")[bass.ds((2 * t + i) * P, P), :])\
                      .then_inc(ctx_arrived[i], 16)

            load_ctx(1)
            for u in range(2, SHARED_UNITS):
                sp.wait_ge(g_wlo, u - 1)
                load_unit(u % 2, *shared(u))
            with sp.Fori(2, B // 2) as t:
                load_ctx(t)
            for u in range(SHARED_UNITS, SHARED_UNITS + 2):
                wait(sp, g_wlo, u - 1)
                load_unit(u % 2, *experts(u))
            for h in range(2):
                sp.wait_ge(v_gate, gate_step(("combine weights by expert", h)))
                sp.dma_start(c_dram[:, h * HALF:(h + 1) * HALF], cT[:, h * HALF:(h + 1) * HALF]).then_inc(c_out[h], 16)
                sp.wait_ge(c_out[h], 16)
                for k in range(2):
                    sp.dma_start(cb[0][k * F:(k + 1) * F, h * HALF:(h + 1) * HALF],
                                 c_dram[k:k + 1, h * HALF:(h + 1) * HALF].broadcast_to([F, HALF])).then_inc((cb_first, cb_in[0])[h], 16)
            load_combine(1, SHARED_UNITS + 1)
            with sp.Fori((SHARED_UNITS + 2) // 2, (UNITS) // 2) as t:
                u = 2 * t
                for i in range(2):
                    sp.wait_ge(g_wlo, u + i - 1)
                    load_unit(i, *experts(u + i))
                    sp.wait_ge(v_h, 2 * (u + i) - 2)
                    load_combine(i, u + i)
            for q in range(4):
                sp.wait_ge(v_y, q + 1)
                sp.dma_start(out[2 * q:2 * q + 2].rearrange("b p d -> p b d"),
                             y[:, 2 * q * D:(2 * q + 2) * D].rearrange("p (b d) -> p b d", b=2)).then_inc(y_out, 16)
            sp.wait_ge(y_out, 64)

        @block.gpsimd
        def _(pool):
            for tile, value in ((moment_of[:, :, 0], 0.5), (moment_of[:, :, 1], 1.0 / D), (moment_of[:, :, 2], 0.25),
                                (eps[:], EPS), (minus_half[:], -0.5), (zeros[:], 0.0)):
                last = nc.gpsimd.memset(tile, value)
            last.then_inc(g_const, 1)

            add, sub, mul = ALU.add, ALU.subtract, ALU.mult

            def deviations(lo, hi, before):
                r = slice(lo, hi)
                done = [before]

                def step(out_, a, b, op):
                    nc.gpsimd.tensor_tensor(out_, a, b, op).then_inc(g_ln, 1)
                    done[0] = done[0] + 1
                    pool.wait_ge(g_ln, done[0])

                step(terms[:, r, 0:2], stats[:, r, 0, 1:3], stats[:, r, 1, 1:3], add)
                step(apart[:, r], stats[:, r, 0, 1], stats[:, r, 1, 1], sub)
                step(terms[:, r, 2], apart[:, r], apart[:, r], mul)
                step(moments[:, r], terms[:, r], moment_of[:, r], mul)
                step(var[:, r], moments[:, r, 1], moments[:, r, 2], add)
                step(var[:, r], var[:, r], eps[:, r], add)
                step(rstd[:, r], var[:, r], minus_half[:, r], ALU.pow)

            pool.wait_ge(g_const, 1)

            def split(i, w, u, n_raw, used, pairs):
                pool.wait_ge(raw_in[i], n_raw)
                pool.wait_ge(a_whi, 2 * u + 1)
                wait(pool, pe_U, used)
                gu_lo = wlo[w][:, 0:2 * D]
                gu_hi = whi[w][:, 0:2 * D].bitcast(F32)
                gu = raw[i][:, 0:2 * D]
                if pairs:
                    for m in range(2):
                        s = slice(m * D, (m + 1) * D)
                        order = "p (e c f) -> p c e f"
                        nc.gpsimd.tensor_tensor(wlo[w][:, s].rearrange("p (c e f) -> p c e f", c=NC, e=2),
                                                raw[i][:, s].rearrange(order, c=NC, e=2),
                                                whi[w][:, s].bitcast(F32).rearrange("p (c e f) -> p c e f", c=NC, e=2),
                                                ALU.subtract)
                else:
                    nc.gpsimd.tensor_tensor(gu_lo, gu, gu_hi, ALU.subtract)
                pool.wait_ge(a_whi, 2 * u + 2)
                wait(pool, pe_D, used)
                nc.gpsimd.tensor_tensor(wlo[w][:, 2 * D:3 * D], raw[i][:, 2 * D:3 * D],
                                        whi[w][:, 2 * D:3 * D].bitcast(F32), ALU.subtract).then_inc(g_wlo, 1)

            def body(n, odd, has):
                if n_is(n, FIRST_N):
                    pool.wait_ge(v_stats, 1)
                    deviations(0, 1, 0)
                    for i in range(2):
                        strips = Vw[i][:, :, HALF_STRIP:].rearrange("p G (s r) -> p G s r", s=SG)
                        nc.gpsimd.memset(strips[:, :, :, HD:2 * HD], 1.0)
                        nc.gpsimd.memset(strips[:, :, :, HALF_STRIP:], 0.0)
                        nc.gpsimd.memset(Vw[i][:, :, 0:HALF_STRIP], 0.0).then_inc(g_const, 1)
                    for i in range(2):
                        nc.gpsimd.memset(minus_maxima(i, 0, HD).bitcast(F32), 0.0)
                    ones = krep[:].rearrange("p (g r d) -> p g r d", g=GROUPS, r=4)[:, :, 3, :]
                    nc.gpsimd.memset(ones[:, :, 2:HD].bitcast(F32), 0.0)
                    nc.gpsimd.memset(ones[:, :, 0:2].bitcast(F32), 1.0).then_inc(g_const, 1)
                    nc.gpsimd.memset(inv_t[:], 1.0 / T).then_inc(g_const, 1)
                    nc.gpsimd.memset(lb[:, :, E:E + 8], FAR).then_inc(g_const, 1)
                    pool.wait_ge(v_stats, 2)
                    deviations(1, B, LN_STEPS)
                if has(n - 2):
                    k = n - 2
                    pool.wait_ge(v_stats, k + 3)
                    wait(pool, v_x2n, k)
                    deviations(LN2, LN2 + 1, LN_STEPS * (k + 2))
                if has(n) and (not isinstance(n, int) or has(n + 2)):
                    pool.wait_ge(pe_qm1, n + 1)
                    m = minus_maxima(odd, 0, 2)
                    nc.gpsimd.tensor_tensor(m, zeros[:], zeros[:], ALU.add).then_inc(g_clear, 1)
                if n_is(n, 0):
                    pool.wait_ge(x_rest, 16)
                    pool.wait_ge(arrived["bfc"], 16)
                    for b in range(B):
                        nc.gpsimd.tensor_tensor(xb_all[:, b * D:(b + 1) * D], x_all[:, b * D:(b + 1) * D], bfc_b[:],
                                                ALU.add).then_inc(g_xb, 1)
                if isinstance(n, int) and n in SPLIT_AT:
                    for u in SPLIT_AT[n]:
                        split(u % 2, u, u, 48 * (u // 2 + 1), 0, False)

            iterations(pool, body)

            pool.wait_ge(v_gate, gate_step("largest logit"))
            nc.gpsimd.tensor_tensor(ex[:], lg[:], lmax[:].rearrange("p (b a) -> p b a", a=1).broadcast_to([P, B, E]),
                                    ALU.subtract).then_inc(g_gate, 1)
            pool.wait_ge(a_ex, 1)
            for i in range(2):
                split(i, i, SHARED_UNITS + i, 24 * SHARED_UNITS + 48, SHARED_UNITS + i + 1, True)
            with pool.Fori((SHARED_UNITS + 2) // 2, (UNITS) // 2) as t:
                u = 2 * t
                for i in range(2):
                    split(i, i, u + i, 24 * u + 48, 2 * (u + i) - 2, True)

        @block.scalar
        def _(act):
            copy, exp = ACT.Copy, ACT.Exp
            act.wait_ge(pe_w, 2)
            nc.scalar.activation(wkvT[:], bank[1][:, 0:NC * P], copy).then_inc(a_w, 1)

            def weights_hi(i, w, n_raw, used, pairs):
                act.wait_ge(raw_in[i], n_raw)
                wait(act, pe_U, used)
                for m in range(2):
                    s = slice(m * D, (m + 1) * D)
                    if pairs:
                        ins = nc.scalar.activation(whi[w][:, s].rearrange("p (c e f) -> p c e f", c=NC, e=2),
                                                   raw[i][:, s].rearrange("p (e c f) -> p c e f", c=NC, e=2), copy)
                    else:
                        ins = nc.scalar.activation(whi[w][:, s], raw[i][:, s], copy)
                ins.then_inc(a_whi, 1)
                wait(act, pe_D, used)
                nc.scalar.activation(whi[w][:, 2 * D:], raw[i][:, 2 * D:], copy).then_inc(a_whi, 1)

            def silu(v, i):
                act.wait_ge(pe_G, v + 1)
                wait(act, v_su, v - 1)
                nc.scalar.activation(sil[i][:], G_ps[:], ACT.Silu).then_inc(a_sil, 1)

            def hidden_hi(v, i):
                act.wait_ge(v_h, v + 1)
                wait(act, pe_D, v - 1)
                nc.scalar.activation(hhi[i][:], hh[i][:], copy).then_inc(a_hhi, 1)

            def body(n, odd, has):
                if has(n + 1):
                    k = n + 1
                    act.wait_ge(pe_QKT, 3 * k + 1)
                    wait(act, pe_ST, 8 * k - 8)
                    if isinstance(k, int) and k < 2:
                        act.wait_ge(v_zero, k + 1)
                    for s in range(SG):
                        last = nc.scalar.activation(
                            kT[1 - odd][s * STRIP:(s + 1) * STRIP, :].rearrange("p (G s t) -> p G s t", G=NG, s=SG)[:, :, s, :],
                            S_ps[0][s * STRIP:(s + 1) * STRIP, 0:NG * T].rearrange("p (G t) -> p G t", G=NG), copy)
                    last.then_inc(a_kT, 1)
                    act.wait_ge(pe_QKT, 3 * k + 2)
                    nc.scalar.activation(qT[1 - odd][:, 0:J * T], MA[:], copy).then_inc(a_qT, 1)
                for g in range(GROUPS):
                    if has(n):
                        act.wait_ge(pe_ST, 8 * n + g + 1)
                        wait(act, pe_PV, 2 * n - 1 + g // SG)
                        nc.scalar.activation(Pr[g], ST_ps[g % 2][:], exp, scale=SCALE).then_inc(a_exp, 1)
                    if isinstance(n, int) and n in SPLIT_AT and g == (4 if n < 0 else 7):
                        for u in SPLIT_AT[n]:
                            weights_hi(u % 2, u, 48 * (u // 2 + 1), 0, False)
                    if g == 1 and has(n):
                        act.wait_ge(pe_qm1, n + 1)
                        nc.scalar.activation(qT[odd][:, J * T:], O_ps[1][:], copy).then_inc(a_qm, 1)
                    if g == 0 and has(n - 1):
                        evac_O(n - 1)
                    if g == 3 and (n_is(n, B) or n_is(n, B + 1)):
                        silu(n - B, (n - B) % 2)
                        hidden_hi(n - B, (n - B) % 2)
                    if g == 2 and has(n + 1):
                        k = n + 1
                        if isinstance(k, int) and k < 2:
                            act.wait_ge(g_const, 3)
                        act.wait_ge(a_qkv, k + 1)
                        nc.scalar.activation(
                            Vw[1 - odd][:, :, HALF_STRIP:].rearrange("p G (s r) -> p G s r", s=SG)[:, :, :, 0:HD],
                            v_sb[:].rearrange("p (G s d) -> p G s d", G=NG, s=SG), copy).then_inc(a_V, 1)
                    if g == 3 and has(n + 2):
                        k = n + 2
                        act.wait_ge(pe_T1, k + 1)
                        wait(act, pe_PJ, k)
                        nc.scalar.activation(xcT[:], O_ps[0][:], copy).then_inc(a_xcT, 1)
                    if g == 4 and has(n - 2):
                        k = n - 2
                        act.wait_ge(pe_XT, k + 1)
                        nc.scalar.activation(xmT[:, :, bass.ds(k, 1)], O_ps[1][:, D:D + NC].rearrange("p (c a) -> p c a", a=1), copy)
                        nc.scalar.activation(x2hi[:, :, bass.ds(k * T, T)], O_ps[1][:, 0:D].rearrange("p (c t) -> p c t", c=NC),
                                             copy).then_inc(a_x2hi, 1)
                    if g == 4 and has(n - 1):
                        act.wait_ge(pe_AT, n)
                        wait(act, pe_FC, n - 1)
                        nc.scalar.activation(attnT[:], MB[:, 0:D], copy).then_inc(a_attnT, 1)
                    if g == 5 and has(n + 2):
                        k = n + 2
                        act.wait_ge(pe_PJ, k + 1)
                        wait(act, pe_QKT, 3 * k)
                        wait(act, a_V, k)
                        nc.scalar.activation(v_sb[:], MA[:, D + 64:D + 128], copy)
                        kv = krep[:].rearrange("p (g r d) -> p g r d", g=GROUPS, r=4)
                        nc.scalar.activation(kv[:, :, 0:2, :],
                                             MA[:, D:D + 64].rearrange("p (g a d) -> p g a d", g=GROUPS, a=1)
                                             .broadcast_to([P, GROUPS, 2, HD]), copy)
                        qv = qrep[odd][:].rearrange("p (h r d) -> p h r d", h=HEADS, r=4)
                        nc.scalar.activation(qv[:, :, 0:4:2, :],
                                             MA[:, 0:D].rearrange("p (h a d) -> p h a d", h=HEADS, a=1)
                                             .broadcast_to([P, HEADS, 2, HD]), copy).then_inc(a_qkv, 1)
                    if g == 7 and n_is(n, -2):
                        act.wait_ge(pe_w, 3)
                        nc.scalar.activation(wfcT[:], MB[:], copy).then_inc(a_w, 1)

            def evac_O(k):
                act.wait_ge(pe_PV, 2 * k + 2)
                wait(act, pe_OT, k)
                nc.scalar.activation(O_sb[:], O_ps[0][:], copy).then_inc(a_O, 1)

            iterations(act, body)

            silu(2, 0)
            act.wait_ge(pe_h1, 1)
            act.wait_ge(arrived["b1"], 16)
            nc.scalar.activation(h1T[:], MA[:, 0:B], ACT.Gelu, bias=b1_c[:, 0:1]).then_inc(a_h1, 1)
            hidden_hi(2, 0)
            act.wait_ge(v_gate, gate_step("domain logits less their maximum"))
            nc.scalar.activation(td[:], td[:], exp, accum_out=tds[:, 0:1]).then_inc(a_td, 1)
            for v in range(EARLY, SHARED_STEPS):
                silu(v, v % 2)
                if v == 3:
                    for i in range(2):
                        act.wait_ge(pe_lg, i + 1)
                        nc.scalar.activation(lg_hi[:, i * B // 2:(i + 1) * B // 2, :],
                                             ACC[1][i][:].rearrange("p (b m e) -> p b m e", b=B // 2, m=2)[:, :, 0, :],
                                             copy).then_inc(a_lg, 1)
                if v == 5:
                    act.wait_ge(g_gate, 1)
                    nc.scalar.activation(ex[:], ex[:], exp).then_inc(a_ex, 1)
                hidden_hi(v, v % 2)
                if v == SHARED_STEPS - 2:
                    weights_hi(0, 0, 24 * SHARED_UNITS + 48, SHARED_UNITS + 1, True)
            def two_units(u, used_second):
                for i in range(2):
                    for half in range(2):
                        v = 2 * (u + i) + half
                        silu(v, half)
                        if half == 0:
                            weights_hi(1 - i, 1 - i, 24 * (u + 2 * i) + 48, 2 * (u + i) if i else used_second, True)
                        hidden_hi(v, half)

            two_units(SHARED_UNITS, SHARED_UNITS + 2)
            with act.Fori((SHARED_UNITS + 2) // 2, (UNITS - 2) // 2) as t:
                two_units(2 * t, 4 * t)
            for u in range(UNITS - 2, UNITS):
                for half in range(2):
                    silu(2 * u + half, half)
                    if half == 0 and u + 1 < UNITS:
                        weights_hi(1, 1, 24 * (UNITS - 2) + 48, 2 * u, True)
                    hidden_hi(2 * u + half, half)
            for half in range(2):
                act.wait_ge(pe_D, 2 * UNITS - 1 + half)
                nc.scalar.activation(yT[:, 0, half * HALF:(half + 1) * HALF], ACC[half][0][:], copy).then_inc(a_yT, 1)

        @block.vector
        def _(dve):
            for i in range(2):
                nc.vector.memset(kT[i][:].bitcast(F32), 0.0).then_inc(v_zero, 1)



            def statistics(slot, row):
                return nc.vector.bn_stats(stats[:, slot].rearrange("p a s -> p (a s)"), row)

            def query_weights():
                dve.wait_ge(pe_w, 1)
                for cG in range(NC * NG):
                    last = nc.vector.tensor_copy(wqT[:, cG * P:(cG + 1) * P].rearrange("p (j s d) -> p j s d", j=J, s=SG),
                                                 bank[0][:, cG * P:(cG + 1) * P].rearrange("p (s j d) -> p j s d", j=J, s=SG))
                last.then_inc(v_w, 1)

            def layernorm(slot, src, dst, done):
                nc.vector.tensor_scalar(dst, src, moments[:, bass.ds(slot, 1), 0], rstd[:, bass.ds(slot, 1)],
                                        ALU.subtract, ALU.mult).then_inc(done, 1)

            def maximum(k, par, g):
                dve.wait_ge(pe_S, 8 * k + g + 1)
                nc.vector.tensor_reduce(mx[par][:, J * g:J * g + J], S_ps[g % 2][:].rearrange("p (j t) -> p j t", j=J),
                                        AX_X, ALU.max).then_inc(v_max, 1)

            def normalise(k):
                dve.wait_ge(pe_OT, k + 1)
                nc.vector.reciprocal(rec[:].rearrange("p (q a) -> p q a", a=1),
                                     MA[:].rearrange("p (q r) -> p q r", r=HALF_STRIP)[:, :, HD:HD + 1]).then_inc(v_rec, 1)
                dve.wait_ge(v_rec, k + 1)
                wait(dve, pe_AT, k)
                for G in range(NG):
                    last = nc.vector.tensor_tensor(
                        attn[:, G * P:(G + 1) * P].rearrange("p (s j d) -> p j s d", s=SG, j=J),
                        MA[:].rearrange("p (j s r) -> p j s r", j=J, s=SG)[:, :, :, G * HALF_STRIP:G * HALF_STRIP + HD],
                        rec[:].rearrange("p (j s G) -> p j s G", j=J, s=SG)[:, :, :, G:G + 1].broadcast_to([P, J, SG, HD]),
                        ALU.mult)
                last.then_inc(v_norm, 1)

            def hidden(v, h, c=None, n_cb=None):
                dve.wait_ge(pe_U, v + 1)
                dve.wait_ge(a_sil, v + 1)
                if c is None:
                    nc.vector.tensor_tensor(hh[h][:], U_ps[:], sil[h][:], ALU.mult).then_inc(v_su, 1)
                    dve.wait_ge(v_su, v + 1)
                    nc.vector.engine_nop().then_inc(v_h, 1)
                else:
                    nc.vector.tensor_tensor(su[h][:], U_ps[:], sil[h][:], ALU.mult).then_inc(v_su, 1)
                    dve.wait_ge(v_su, v + 1)
                    dve.wait_ge(cb_first if n_is(v, SHARED_STEPS) else cb_in[c], n_cb)
                    nc.vector.tensor_tensor(hh[h][:], su[h][:], cb[c][:, h * HALF:(h + 1) * HALF],
                                            ALU.mult).then_inc(v_h, 1)

            def hidden_low(v, h):
                dve.wait_ge(a_hhi, v + 1)
                nc.vector.tensor_tensor(hlo[h][:], hh[h][:], hhi[h][:].bitcast(F32), ALU.subtract).then_inc(v_hlo, 1)

            def body(n, odd, has):
                k1 = n + 1
                if n_is(n, FIRST_N):
                    dve.wait_ge(x_first, 16)
                    statistics(0, x_all[:, 0:D]).then_inc(v_stats, 1)
                if has(n - 2):
                    k = n - 2
                    dve.wait_ge(x_rest, 16)
                    wait(dve, g_ln, LN_STEPS * (k + 2))
                    dve.wait_ge(v_x2, k + 1)
                    statistics(LN2, xb_all[:, bass.ds(k * D, D)]).then_inc(v_stats, 1)
                if has(n):
                    dve.wait_ge(pe_qm0, n + 1)
                    nc.vector.tensor_copy(qT[odd][:, 0:J * T], S_ps[1][:]).then_inc(v_qm, 1)
                if has(n + 2):
                    k = n + 2
                    dve.wait_ge(g_ln, LN_STEPS * (1 if n_is(k, 0) else 2))
                    wait(dve, pe_T1, k)
                    layernorm(k, x_all[:, bass.ds(k * D, D)], xn[:], v_xn)
                if has(k1):
                    dve.wait_ge(pe_QKT, 3 * k1 + 3)
                    wait(dve, pe_ST, 8 * k1 - 8)
                    nc.vector.tensor_copy(qT[1 - odd][:, J * T:], MB[:]).then_inc(v_qT, 1)
                for g in range(GROUPS):
                    if g == 2 and has(n - 1):
                        normalise(n - 1)
                    if g == 2 and n_is(n, FIRST_N):
                        query_weights()
                        dve.wait_ge(arrived["ident"], 16)
                        nc.vector.tensor_copy(ident_r[:], ident[:]).then_inc(v_ident, 1)
                        dve.wait_ge(x_rest, 16)
                        for b in range(1, B):
                            last = statistics(b, x_all[:, b * D:(b + 1) * D])
                        last.then_inc(v_stats, 1)
                    if g == 3 and n_is(n, -1):
                        dve.wait_ge(pe_w, 4)
                        nc.vector.tensor_copy(wrT[:], O_ps[1][:, 0:NC * E]).then_inc(v_w, 1)
                        dve.wait_ge(v_w, 2)
                        w = wrT[:].rearrange("p (c e) -> p c e", c=NC)
                        nc.vector.tensor_copy(wrT_hl[:, :, 0, :], w).then_inc(v_w, 1)
                        dve.wait_ge(v_w, 3)
                        nc.vector.tensor_tensor(wrT_hl[:, :, 1, :], w, wrT_hl[:, :, 0, :].bitcast(F32), ALU.subtract).then_inc(v_w, 1)
                        nc.vector.tensor_copy(w1T[:], O_ps[1][:, P:P + NC * P])
                        nc.vector.tensor_copy(w2T[:], O_ps[1][:, P + NC * P:P + NC * P + ND])
                        nc.vector.tensor_copy(affT[:], O_ps[1][0:ND, P + NC * P + 64:P + NC * P + 64 + E]).then_inc(v_w, 1)
                    if g == 1 and n_is(n, B + 1):
                        hidden(1, 1)
                    if g == 2 and n_is(n, B + 1):
                        hidden_low(1, 1)
                    if g == 3 and n_is(n, B):
                        hidden(0, 0)
                        hidden_low(0, 0)
                    if has(k1):
                        for i in SCORES_AT[g]:
                            maximum(k1, 1 - odd, i)
                    if g == 1 and has(n - 2):
                        k = n - 2
                        dve.wait_ge(g_ln, LN_STEPS * (k + 3))
                        wait(dve, pe_XT, k)
                        layernorm(LN2, xb_all[:, bass.ds(k * D, D)], x2n[:], v_x2n)
                    if g == 4 and has(n - 2):
                        k = n - 2
                        dve.wait_ge(a_x2hi, k + 1)
                        nc.vector.tensor_tensor(x2lo[:, :, bass.ds(k * T, T)], O_ps[1][:, 0:D].rearrange("p (c t) -> p c t", c=NC),
                                                x2hi[:, :, bass.ds(k * T, T)].bitcast(F32), ALU.subtract).then_inc(v_x2lo, 1)
                    if g == 5 and has(n + 2):
                        k = n + 2
                        dve.wait_ge(a_qkv, k + 1)
                        kv = krep[:].rearrange("p (g r d) -> p g r d", g=GROUPS, r=4)
                        nc.vector.tensor_tensor(kv[:, :, 2, :], MA[:, D:D + 64].rearrange("p (g d) -> p g d", g=GROUPS),
                                                kv[:, :, 0, :].bitcast(F32), ALU.subtract)
                        qv = qrep[odd][:].rearrange("p (h r d) -> p h r d", h=HEADS, r=4)
                        nc.vector.tensor_tensor(qv[:, :, 1, :], MA[:, 0:D].rearrange("p (h d) -> p h d", h=HEADS),
                                                qv[:, :, 0, :].bitcast(F32), ALU.subtract).then_inc(v_lo, 1)
                if has(k1):
                    dve.wait_ge(v_max, 8 * k1 + 8)
                    m = mx[1 - odd][:].rearrange("p (h a) -> p h a", a=1)
                    hi, lo = minus_maxima(1 - odd, 0, 1), minus_maxima(1 - odd, 1, 2)
                    nc.vector.tensor_scalar(hi, m, -1.0, None, ALU.mult).then_inc(v_mhi, 1)
                    dve.wait_ge(v_mhi, k1 + 1)
                    nc.vector.scalar_tensor_tensor(out=lo, in0=m, scalar=-1.0, in1=hi.bitcast(F32),
                                                   op0=ALU.mult, op1=ALU.subtract).then_inc(v_ml, 1)
                if has(n - 1):
                    k = n - 1
                    dve.wait_ge(pe_FC, k + 1)
                    if isinstance(k, int) and k == 0:
                        dve.wait_ge(g_xb, B)
                    row = xb_all[:, bass.ds(k * D, D)]
                    nc.vector.tensor_tensor(row, MB[:, 0:D], row, ALU.add).then_inc(v_x2, 1)

            iterations(dve, body)

            steps = []

            def step(name, ins):
                steps.append(name)
                ins.then_inc(v_gate, 1)
                dve.wait_ge(v_gate, gate_step(name))

            def logits_sum():
                for i in range(2):
                    b = slice(i * B // 2, (i + 1) * B // 2)
                    dve.wait_ge(a_lg, i + 1)
                    last = nc.vector.tensor_tensor(lg[:, b, :], ACC[1][i][:].rearrange("p (b m e) -> p b m e", b=B // 2, m=2)[:, :, 1, :],
                                                   lg_hi[:, b, :], ALU.add)
                step("logits without the domains' share", last)

            def domains_in():
                dve.wait_ge(pe_td, 1)
                dve.wait_ge(arrived["b2"], 16)
                step("domain logits", nc.vector.tensor_tensor(td[:], MB[0:B, 0:ND], b2_b[:], ALU.add))
                step("their maximum", nc.vector.tensor_reduce(tdm[:], td[:], AX_X, ALU.max))
                step("domain logits less their maximum", nc.vector.tensor_scalar(td[:], td[:], tdm[:, 0:1], None, ALU.subtract))

            def domains_out():
                dve.wait_ge(a_td, 1)
                step("one over the domains' sum", nc.vector.reciprocal(tdr[:], tds[:]))
                step("half the domain shares", nc.vector.tensor_scalar(tdn[:], td[:], tdr[:, 0:1], 0.5, ALU.mult, ALU.mult))

            def domains_spread():
                dve.wait_ge(pe_tdT, 1)
                step("shares by domain", nc.vector.tensor_copy(tdT[:], MA[0:ND, 0:B]))
                step("shares for every token", nc.vector.tensor_copy(
                    tdb[:].rearrange("p (b t) -> p b t", b=B), tdT[:].rearrange("p (b a) -> p b a", a=1).broadcast_to([ND, B, T])))

            def logits_whole():
                dve.wait_ge(pe_dom, 1)
                dve.wait_ge(arrived["rbias"], 16)
                step("logits", nc.vector.tensor_tensor(lg[:], MB[:].rearrange("p (b e) -> p b e", b=B), lg[:], ALU.add))
                step("largest logit", nc.vector.tensor_reduce(lmax[:], lg[:], AX_X, ALU.max))

            def batches(h):
                return slice(h * B // 2, (h + 1) * B // 2)

            def over_experts(per_token):
                return per_token.rearrange("p (b a) -> p b a", a=1).broadcast_to([P, B // 2, E])

            def largest_biased(h):
                r = batches(h)
                step(("logits with bias", h), nc.vector.tensor_tensor(
                    lb[:, r, 0:E], lg[:, r], rbias_b[:].rearrange("p (a e) -> p a e", a=1).broadcast_to([P, B // 2, E]), ALU.add))
                for b in range(r.start, r.stop):
                    ins = nc.vector.max(top[:, b, :], lb[:, b, 0:E])
                step(("eight largest", h), ins)
                step(("four largest and fillers", h), nc.vector.memset(top[:, r, TOPK:8], FAR))

            def chosen(h):
                r = batches(h)
                for b in range(r.start, r.stop):
                    ins = nc.vector.match_replace(rep[:, b, :], top[:, b, :], lb[:, b, :], -FAR)
                step(("four largest struck out", h), ins)
                step(("chosen", h), nc.vector.tensor_tensor(sel[:, r], rep[:, r, 0:E], lb[:, r, 0:E], ALU.not_equal))

            def combine(h):
                r = batches(h)
                dve.wait_ge(a_ex, 1)
                step(("sum of exp", h), nc.vector.tensor_reduce(z_all[:, r], ex[:, r], AX_X, ALU.add))
                step(("exp of the chosen", h), nc.vector.tensor_tensor(ex[:, r], ex[:, r], sel[:, r], ALU.mult))
                step(("their sum", h), nc.vector.tensor_reduce(z_top[:, r], ex[:, r], AX_X, ALU.add))
                step(("guarded sum", h), nc.vector.scalar_tensor_tensor(out=z_all[:, r], in0=z_all[:, r], scalar=GUARD,
                                                                        in1=z_top[:, r], op0=ALU.mult, op1=ALU.add))
                step(("one over it", h), nc.vector.reciprocal(z_top[:, r], z_all[:, r]))
                step(("combine weights", h), nc.vector.tensor_tensor(cw[:, r], ex[:, r], over_experts(z_top[:, r]), ALU.mult))

            def combine_by_expert(h):
                dve.wait_ge(pe_cT, h + 1)
                step(("combine weights by expert", h), nc.vector.tensor_copy(cT[:, h * HALF:(h + 1) * HALF], (MA, MB)[h][0:E, :]))

            hidden(2, 0)
            hidden_low(2, 0)
            domains_in()
            domains_out()
            hidden(3, 1)
            logits_sum()
            domains_spread()
            hidden_low(3, 1)
            dve.wait_ge(g_const, 6)
            logits_whole()
            hidden(4, 0)
            largest_biased(0)
            hidden_low(4, 0)
            chosen(0)
            hidden(5, 1)
            largest_biased(1)
            hidden_low(5, 1)
            combine(0)
            hidden(6, 0)
            combine_by_expert(0)
            chosen(1)
            hidden_low(6, 0)
            hidden(7, 1)
            combine(1)
            hidden_low(7, 1)
            combine_by_expert(1)
            assert tuple(steps) == GATE, steps

            def two_units(u):
                for i in range(2):
                    for half in range(2):
                        v = 2 * (u + i) + half
                        hidden(v, half, i, 16 * (u - SHARED_UNITS) + 32)
                        hidden_low(v, half)

            two_units(SHARED_UNITS)
            with dve.Fori((SHARED_UNITS + 2) // 2, (UNITS) // 2) as t:
                two_units(2 * t)
            for half in range(2):
                dve.wait_ge(pe_D, 2 * UNITS - 1 + half)
                nc.vector.tensor_copy(yT[:, 1, half * HALF:(half + 1) * HALF], ACC[half][1][:]).then_inc(v_yT, 1)
            for q in range(4):
                dve.wait_ge(pe_Y, q + 1)
                nc.vector.tensor_tensor(y[:, 2 * q * D:(2 * q + 2) * D], Y_ps[q][:],
                                        xb_all[:, 2 * q * D:(2 * q + 2) * D], ALU.add).then_inc(v_y, 1)

        @block.tensor
        def _(pe):
            mm = nc.tensor.matmul

            def turn(out_, in_):
                k = in_.shape[0]
                return nc.tensor.transpose(out_, in_, ident[0:k, 0:k])

            def turn_parts(out_, in_):
                return nc.tensor.transpose(out_.bitcast(F32R), in_, ident_r[:])

            pe.wait_ge(arrived["ident"], 16)
            pe.wait_ge(arrived["wq"], 16)
            for c in range(NC):
                for a in range(NC):
                    last = turn(bank[0][:, (c * NC + a) * P:(c * NC + a + 1) * P], wq_n[:, a, c * P:(c + 1) * P])
            last.then_inc(pe_w, 1)
            pe.wait_ge(arrived["wkv"], 32)
            for c in range(NC):
                last = turn(bank[1][:, c * P:(c + 1) * P], wkv_n[:, c * P:(c + 1) * P])
            last.then_inc(pe_w, 1)

            def output_weights():
                pe.wait_ge(arrived["wfc"], 16)
                for c in range(NC):
                    for a in range(NC):
                        last = turn(MB[:, (c * NC + a) * P:(c * NC + a + 1) * P], wfc_n[:, a, c * P:(c + 1) * P])
                last.then_inc(pe_w, 1)

            def gate_weights():
                for n_ in ("wr", "w1", "w2", "aff"):
                    pe.wait_ge(arrived[n_], 16)
                for c in range(NC):
                    turn(O_ps[1][:, c * E:(c + 1) * E], wr_n[:, c:D:NC])
                for c in range(NC):
                    turn(O_ps[1][:, P + c * P:P + (c + 1) * P], w1_n[:, c:D:NC])
                turn(O_ps[1][:, P + NC * P:P + NC * P + ND], w2_n[:])
                turn(O_ps[1][0:ND, P + NC * P + 64:P + NC * P + 64 + E], aff_n[:]).then_inc(pe_w, 1)

            def rows(s):
                return slice(s * STRIP, (s + 1) * STRIP)

            def product(out_, w_hi, w_lo, r_hi, r_lo, chunks, first, last_):
                n_ = 3 * len(chunks)
                i = 0
                for c in chunks:
                    for w, r in ((w_hi, r_hi), (w_hi, r_lo), (w_lo, r_hi)):
                        ins = mm(out_, w(c), r(c), start=(first and i == 0), stop=(last_ and i == n_ - 1))
                        i += 1
                return ins

            def gate_or_up(v, half, i, m):
                t = slice(half * HALF, (half + 1) * HALF)
                bank_, free, done = ((G_ps, a_sil, pe_G), (U_ps, v_su, pe_U))[m]
                wait(pe, free, v)
                product(bank_[:], lambda c: whi[i][:, m * D + c * P:m * D + (c + 1) * P],
                        lambda c: wlo[i][:, m * D + c * P:m * D + (c + 1) * P],
                        lambda c: x2hi[:, c, t], lambda c: x2lo[:, c, t], range(NC), True, True).then_inc(done, 1)

            def down(v, half, i, h, first=False, last_=False):
                pe.wait_ge(v_hlo, v + 1)
                for dh in range(NC):
                    ins = product(ACC[half][dh][:], lambda c: whi[i][:, 2 * D + dh * P:2 * D + (dh + 1) * P],
                                  lambda c: wlo[i][:, 2 * D + dh * P:2 * D + (dh + 1) * P],
                                  lambda c: hhi[h][:], lambda c: hlo[h][:], range(1), first, last_)
                ins.then_inc(pe_D, 1)

            def domains_hidden():
                pe.wait_ge(a_x2hi, B)
                for c in range(NC):
                    last = mm(MA[:, 0:B], w1T[:, c * P:(c + 1) * P], xmT[:, c, :], start=(c == 0), stop=(c == NC - 1))
                last.then_inc(pe_h1, 1)

            def shared_gate(v):
                half, u = divmod(v, SHARED_UNITS)
                if half == 0:
                    pe.wait_ge(g_wlo, u + 1)
                gate_or_up(v, half, u, 0)

            def shared_up(v):
                half, u = divmod(v, SHARED_UNITS)
                gate_or_up(v, half, u, 1)

            def shared_down(v):
                half, u = divmod(v, SHARED_UNITS)
                if v == SHARED_UNITS:
                    pe.wait_ge(v_gate, gate_step("logits without the domains' share"))
                down(v, half, u, v % 2, first=(u == 0))

            def body(n, odd, has):
                def scores_by_query(i):
                    k, G, o = n + 1, i // J, 1 - odd
                    if i == 0:
                        pe.wait_ge(a_kT, k + 1)
                        pe.wait_ge(a_qT, k + 1)
                    if i == 1:
                        wait(pe, v_qm, k)
                    if i == J:
                        pe.wait_ge(v_qT, k + 1)
                    if i > 1:
                        pe.wait_ge(v_max, 8 * k + i - 1)
                    mm(S_ps[i % 2][:], qT[o][:, i * T:(i + 1) * T], kT[o][:, G * SG * T:(G + 1) * SG * T],
                       start=True, stop=True).then_inc(pe_S, 1)

                def scores_by_key(g):
                    G = g // SG
                    if g == 0:
                        pe.wait_ge(v_qm, n + 1)
                    if g == SG:
                        pe.wait_ge(a_qm, n + 1)
                    wait(pe, a_exp, 8 * n + g - 1)
                    mm(ST_ps[g % 2][:], kT[odd][:, g * T:(g + 1) * T], qT[odd][:, G * J * T:(G + 1) * J * T],
                       start=True, stop=True).then_inc(pe_ST, 1)

                def values(k, par, G):
                    pe.wait_ge(a_V, k + 1)
                    pe.wait_ge(a_exp, 8 * k + SG * G + SG)
                    if G == 0:
                        wait(pe, a_O, k)
                    for s in range(SG):
                        c = HALF_STRIP * (1 - G) + s * STRIP
                        last = mm(O_ps[0][rows(s), :], Vw[par][:, G, c:c + STRIP], Pr[SG * G + s],
                                  start=(G == 0), stop=(G == NG - 1))
                    last.then_inc(pe_PV, 1)

                def heads_by_query(k):
                    pe.wait_ge(a_O, k + 1)
                    for j in range(J):
                        last = turn(MA[:, j * P:(j + 1) * P], O_sb[:, j * T:(j + 1) * T])
                    last.then_inc(pe_OT, 1)

                def turn_queries(out_, i, G):
                    for j in range(J):
                        last = turn_parts(out_[:, j * T:(j + 1) * T], qrep[i][:, (G * J + j) * P:(G * J + j + 1) * P])
                    return last

                def query_operand(k, G):
                    turn_queries((MA, MB)[G], 1 - odd, G).then_inc(pe_QKT, 1)

                if has(n + 1):
                    k = n + 1
                    pe.wait_ge(v_lo, k + 1)
                    wait(pe, g_clear, k - 1)
                    if n_is(k, 0):
                        pe.wait_ge(v_ident, 1)
                        pe.wait_ge(g_const, 4)
                    wait(pe, v_max, 8 * k - 1)
                    for G in range(NG):
                        last = turn_parts(S_ps[0][:, G * T:(G + 1) * T], krep[:, G * P:(G + 1) * P])
                    last.then_inc(pe_QKT, 1)
                    query_operand(k, 0)
                if has(n):
                    pe.wait_ge(v_ml, n + 1)
                    turn_queries(S_ps[1], odd, 0).then_inc(pe_qm0, 1)
                    if n_is(n, 0):
                        pe.wait_ge(v_w, 5)
                    wait(pe, v_x2lo, n - 2)
                    turn_queries(O_ps[1], odd, 1).then_inc(pe_qm1, 1)
                if has(n - 1):
                    values(n - 1, 1 - odd, 1)
                if n_is(n, B):
                    shared_gate(0)
                    shared_up(0)
                if has(n + 1):
                    wait(pe, v_x2, n - 1)
                    if n_is(n, -1):
                        pe.wait_ge(a_w, 2)
                    query_operand(n + 1, 1)

                def scores(g):
                    if has(n + 1):
                        for i in SCORES_AT[g]:
                            scores_by_query(i)

                for g in range(GROUPS):
                    if has(n):
                        scores_by_key(g)
                    if g == 2 and has(n - 1):
                        if has(n + 1):
                            pe.wait_ge(a_qT, n + 2)
                        heads_by_query(n - 1)
                    if g == 4 and n_is(n, B + 1):
                        shared_gate(2)
                        shared_up(2)
                    if g == 3 and has(n + 2):
                        k = n + 2
                        pe.wait_ge(ctx_arrived[odd], 8 * (k - odd) + 16)
                        if has(n - 1):
                            pe.wait_ge(a_O, n)
                        pe.wait_ge(v_xn, k + 1)
                        for c in range(NC):
                            turn(O_ps[0][:, c * T:(c + 1) * T], xn[:, c * P:(c + 1) * P])
                        for c in range(NC):
                            last = turn(O_ps[0][:, D + c * T:D + (c + 1) * T], ctx_in[odd][:, c * P:(c + 1) * P])
                        last.then_inc(pe_T1, 1)
                    if g == 4 and has(n - 2):
                        k = n - 2
                        pe.wait_ge(v_x2n, k + 1)
                        if isinstance(k, int) and k == 0:
                            pe.wait_ge(g_const, 5)
                        if has(n):
                            pe.wait_ge(a_qm, n + 1)
                        else:
                            pe.wait_ge(v_x2lo, n - 2)
                        for c in range(NC):
                            turn(O_ps[1][:, c * T:(c + 1) * T], x2n[:, c:D:NC])
                        for c in range(NC):
                            last = mm(O_ps[1][:, D + c:D + c + 1], x2n[:, c:D:NC], inv_t[:, 0:1], start=True, stop=True)
                        last.then_inc(pe_XT, 1)
                        if n_is(n, B + 1):
                            shared_down(1)
                            domains_hidden()
                    if g == 4 and n_is(n, B):
                        shared_gate(1)
                    if g == 4 and has(n - 1):
                        pe.wait_ge(v_norm, n)
                        if has(n + 1):
                            pe.wait_ge(v_qT, n + 2)
                        else:
                            pe.wait_ge(v_x2, n - 1)
                        for c in range(NC):
                            last = turn(MB[:, c * T:(c + 1) * T], attn[:, c * P:(c + 1) * P])
                        last.then_inc(pe_AT, 1)
                    if g == 5 and has(n + 2):
                        k = n + 2
                        pe.wait_ge(a_xcT, k + 1)
                        if n_is(k, 0):
                            pe.wait_ge(v_w, 1)
                            pe.wait_ge(a_w, 1)
                        if has(n - 1):
                            pe.wait_ge(v_norm, n)
                        elif has(n + 1):
                            pe.wait_ge(a_qT, n + 2)
                        for c in range(NC):
                            mm(MA[:, 0:D], xcT[:, c * T:(c + 1) * T], wqT[:, c * D:(c + 1) * D], start=(c == 0), stop=(c == NC - 1))
                        for c in range(NC):
                            last = mm(MA[:, D:D + P], xcT[:, D + c * T:D + (c + 1) * T], wkvT[:, c * P:(c + 1) * P],
                                      start=(c == 0), stop=(c == NC - 1))
                        last.then_inc(pe_PJ, 1)
                    if g == 5:
                        scores(g)
                    if g == 5 and has(n):
                        values(n, odd, 0)
                    if g == 7 and n_is(n, -2):
                        output_weights()
                    if g == 2 and n_is(n, -1):
                        gate_weights()
                    if g == 7 and n_is(n, B):
                        shared_up(1)
                    if g == 7 and has(n - 1):
                        pe.wait_ge(a_attnT, n)
                        for c in range(NC):
                            last = mm(MB[:, 0:D], attnT[:, c * T:(c + 1) * T], wfcT[:, c * D:(c + 1) * D],
                                      start=(c == 0), stop=(c == NC - 1))
                        last.then_inc(pe_FC, 1)
                    if g != 5:
                        scores(g)
                if n_is(n, B):
                    shared_down(0)

            iterations(pe, body)

            def logits():
                pe.wait_ge(v_x2lo, B)
                for b in range(B):
                    o = ACC[1][b // (B // 2)][:, (b % (B // 2)) * 2 * E:(b % (B // 2) + 1) * 2 * E]
                    parts = [(c, xs) for c in range(NC) for xs in (x2hi, x2lo)]
                    for i, (c, xs) in enumerate(parts):
                        last = mm(o, xs[:, c, b * T:(b + 1) * T], wrT_hl[:, c].rearrange("p m e -> p (m e)"),
                                  start=(i == 0), stop=(i == len(parts) - 1))
                    if b % (B // 2) == B // 2 - 1:
                        last.then_inc(pe_lg, 1)

            def domains_logits():
                pe.wait_ge(a_h1, 1)
                mm(MB[0:B, 0:ND], h1T[:], w2T[:], start=True, stop=True).then_inc(pe_td, 1)

            def domains_turn():
                pe.wait_ge(v_gate, gate_step("half the domain shares"))
                turn(MA[0:ND, 0:B], tdn[:]).then_inc(pe_tdT, 1)

            def domains_share():
                pe.wait_ge(v_gate, gate_step("shares for every token"))
                for b in range(B):
                    last = mm(MB[:, b * E:(b + 1) * E], tdb[:, b * T:(b + 1) * T], affT[:], start=True, stop=True)
                last.then_inc(pe_dom, 1)

            def combine_turn(h):
                pe.wait_ge(v_gate, gate_step(("combine weights", h)))
                for i in range(B // 2):
                    last = turn((MA, MB)[h][0:E, i * T:(i + 1) * T], cw[:, h * B // 2 + i, :])
                last.then_inc(pe_cT, 1)

            logits()
            domains_logits()
            gate = {(3, 1): domains_turn, (4, 0): domains_share, (6, 2): lambda: combine_turn(0)}
            for v in range(EARLY, SHARED_STEPS):
                for part, piece in enumerate((shared_gate, shared_up, lambda v: shared_down(v - 1))):
                    piece(v)
                    if (v, part) in gate:
                        gate[v, part]()

            def two_units(u, first=False):
                for i in range(2):
                    pe.wait_ge(g_wlo, u + i + 1)
                    for half in range(2):
                        v = 2 * (u + i) + half
                        gate_or_up(v, half, i, 0)
                        gate_or_up(v, half, i, 1)
                        if first and i + half == 0:
                            combine_turn(1)
                        if first and i + half == 0:
                            shared_down(v - 1)
                        else:
                            down(v - 1, 1 - half, i if half else 1 - i, 1 - half)

            two_units(SHARED_UNITS, first=True)
            with pe.Fori((SHARED_UNITS + 2) // 2, UNITS // 2 - 1) as t:
                two_units(2 * t)
            for i in range(2):
                pe.wait_ge(g_wlo, UNITS - 1 + i)
                for half in range(2):
                    v = 2 * (UNITS - 2 + i) + half
                    for m in range(2):
                        gate_or_up(v, half, i, m)
                    if i == 0:
                        down(v - 1, 1 - half, 1 - half, 1 - half)
            down(2 * UNITS - 3, 1, 0, 1)
            down(2 * UNITS - 2, 0, 1, 0, last_=True)
            down(2 * UNITS - 1, 1, 1, 1, last_=True)
            for q in range(4):
                pe.wait_ge(a_yT, q // 2 + 1)
                pe.wait_ge(v_yT, q // 2 + 1)
                for b in (2 * q, 2 * q + 1):
                    for dh in range(NC):
                        last = turn(Y_ps[q][:, (b % 2) * D + dh * P:(b % 2) * D + (dh + 1) * P],
                                    yT[:, dh, b * T:(b + 1) * T])
                last.then_inc(pe_Y, 1)


_INS = ["x", "ctx_2048", "L0_xattn_Wq", "L0_xattn_Wk", "L0_xattn_Wv", "L0_xattn_Wfc", "L0_xattn_bfc", "L0_ffn_Wr",
        "L0_ffn_router_bias", "L0_ffn_affinity", "L0_ffn_te_W1", "L0_ffn_te_b1", "L0_ffn_te_W2", "L0_ffn_te_b2",
        "L0_ffn_Wg", "L0_ffn_Wu", "L0_ffn_Wd", "L0_ffn_Sg", "L0_ffn_Su", "L0_ffn_Sd"]


def kernel(**inputs):
    import numpy as _np
    import concourse.bacc as _bacc
    from concourse import mybir as _mybir
    from concourse.bass_utils import run_bass_kernel_spmd as _run

    nc = _bacc.Bacc("TRN2", target_bir_lowering=False, num_devices=1)
    arrays = {f"in_{n}": _np.ascontiguousarray(inputs[n]) for n in _INS}
    arrays["const_ident"] = _np.eye(P, dtype=_np.float32)
    args = [nc.dram_tensor(n, a.shape, _mybir.dt.from_np(a.dtype), kind="ExternalInput").ap() for n, a in arrays.items()]
    out = nc.dram_tensor("out_0", (B, T, D), _mybir.dt.float32, kind="ExternalOutput").ap()
    build(nc, *args, out)
    result = _run(nc, [arrays], core_ids=[0])
    return result.results[0]["out_0"]
```
